# Optimizing a Trainium2 kernel written in Bass

```python
import numpy as np
import jax
import jax.numpy as jnp

def _softmax(x, axis=-1):
    return jax.nn.softmax(x, axis=axis)

def _gelu(x):
    return jax.nn.gelu(x, approximate=True)

def _silu(x):
    return jax.nn.silu(x)

def _sigmoid(x):
    return jax.nn.sigmoid(x)

def _layernorm(x, axis=-1, eps=1e-05):
    m = jnp.mean(x, axis=axis, keepdims=True)
    v = jnp.var(x, axis=axis, keepdims=True)
    return (x - m) / jnp.sqrt(v + eps)

def _scatter_add(tgt, idx, src, axis=0):
    return tgt.at[idx].add(src)

def _segment_sum(src, seg, n):
    return jax.ops.segment_sum(src, seg, n)
kernel_name = 'mk_seq_preln_d1_jaxref_r8_fae5c9'

def setup_inputs(seed: int=0):
    np.random.seed(seed)
    _w = jnp.asarray

    def _L0_attn_setup():
        import math
        import jax, jax.numpy as jnp
        import numpy as np
        B, T, D = (2, 256, 256)
        H = 16
        HD = D // H
        key = jax.random.key(seed)
        k1, k2, k3 = jax.random.split(key, 3)
        x = jax.random.normal(k1, (B, T, D), dtype=jnp.float32)
        w_attn = jax.random.normal(k2, (D, 3 * D), dtype=jnp.float32) * (1.0 / math.sqrt(D))
        w_proj = jax.random.normal(k3, (D, D), dtype=jnp.float32) * (1.0 / math.sqrt(D))
        return {'x': x, 'w_attn': w_attn, 'w_proj': w_proj}
    _L0_attn_in = _L0_attn_setup()

    def _L0_ffn_setup():
        import jax, jax.numpy as jnp
        import numpy as np
        from jax import lax
        H = 256
        I = 128
        E = 32
        K = 4
        SH_I = 256
        EPS = 1e-06

        def _rmsnorm(x, w, eps=EPS):
            var = jnp.mean(jnp.square(x.astype(jnp.float32)), axis=-1, keepdims=True)
            return (x * lax.rsqrt(var + eps)).astype(x.dtype) * w
        key = jax.random.key(seed)
        ks = jax.random.split(key, 8)
        s = lambda d: 1.0 / np.sqrt(d)
        return {'x': jax.random.normal(ks[0], (2, 256, H), jnp.float32), 'norm_w': jnp.ones((H,), jnp.float32), 'router_w': jax.random.normal(ks[1], (E, H), jnp.float32) * s(H), 'w1': jax.random.normal(ks[2], (E, H, 2 * I), jnp.float32) * s(H), 'w2': jax.random.normal(ks[3], (E, I, H), jnp.float32) * s(I), 'sg': jax.random.normal(ks[4], (H, SH_I), jnp.float32) * s(H), 'su': jax.random.normal(ks[5], (H, SH_I), jnp.float32) * s(H), 'sd': jax.random.normal(ks[6], (SH_I, H), jnp.float32) * s(SH_I)}
    _L0_ffn_in = _L0_ffn_setup()
    _d = {'L0_attn_x': _L0_attn_in['x'], 'L0_attn_w_attn': _L0_attn_in['w_attn'], 'L0_attn_w_proj': _L0_attn_in['w_proj'], 'L0_ffn_norm_w': _L0_ffn_in['norm_w'], 'L0_ffn_router_w': _L0_ffn_in['router_w'], 'L0_ffn_w1': _L0_ffn_in['w1'], 'L0_ffn_w2': _L0_ffn_in['w2'], 'L0_ffn_sg': _L0_ffn_in['sg'], 'L0_ffn_su': _L0_ffn_in['su'], 'L0_ffn_sd': _L0_ffn_in['sd']}
    _x0 = _d['L0_attn_x']
    _d['L0_attn_x'] = jax.random.normal(jax.random.fold_in(jax.random.key(seed), 1), (1, 1024, 256), dtype=_x0.dtype)
    del _x0
    return _d

def reference(L0_attn_x, L0_attn_w_attn, L0_attn_w_proj, L0_ffn_norm_w, L0_ffn_router_w, L0_ffn_w1, L0_ffn_w2, L0_ffn_sg, L0_ffn_su, L0_ffn_sd):

    def _L0_attn_ref(x, w_attn, w_proj):
        import math
        import jax, jax.numpy as jnp
        import numpy as np
        B, T, D = (2, 256, 256)
        H = 16
        HD = D // H
        Bc, Tc, Dc = x.shape
        qkv = x @ w_attn
        q, k, v = jnp.split(qkv, 3, axis=2)
        q = q.reshape(Bc, Tc, H, HD).transpose(0, 2, 1, 3)
        k = k.reshape(Bc, Tc, H, HD).transpose(0, 2, 1, 3)
        v = v.reshape(Bc, Tc, H, HD).transpose(0, 2, 1, 3)
        att = jnp.einsum('bhqd,bhkd->bhqk', q, k) * (1.0 / math.sqrt(HD))
        causal = jnp.tril(jnp.ones((Tc, Tc), dtype=bool))
        att = jnp.where(causal[None, None], att, -jnp.inf)
        att = jax.nn.softmax(att, axis=-1)
        y = jnp.einsum('bhqk,bhkd->bhqd', att, v)
        y = y.transpose(0, 2, 1, 3).reshape(Bc, Tc, Dc)
        return y @ w_proj

    def _L0_ffn_ref(x, norm_w, router_w, w1, w2, sg, su, sd):
        import jax, jax.numpy as jnp
        import numpy as np
        from jax import lax
        H = 256
        I = 128
        E = 32
        K = 4
        SH_I = 256
        EPS = 1e-06

        def _rmsnorm(x, w, eps=EPS):
            var = jnp.mean(jnp.square(x.astype(jnp.float32)), axis=-1, keepdims=True)
            return (x * lax.rsqrt(var + eps)).astype(x.dtype) * w
        B, S, _ = x.shape
        residual = x
        h = _rmsnorm(x, norm_w)
        flat = h.reshape(-1, H)
        T = flat.shape[0]
        logits = flat.astype(jnp.float32) @ router_w.T
        scores = jax.nn.softmax(logits, axis=-1)
        topk_w, topk_ids = lax.top_k(scores, K)
        topk_w = topk_w / jnp.sum(topk_w, axis=-1, keepdims=True)
        ids = topk_ids.reshape(-1)
        sort_idx = jnp.argsort(ids)
        tok_idx = sort_idx // K
        xs = jnp.take(flat, tok_idx, axis=0)
        group_sizes = jnp.bincount(ids, length=E).astype(jnp.int32)
        gu = lax.ragged_dot(xs, w1, group_sizes)
        g, u = jnp.split(gu, 2, axis=-1)
        act = jax.nn.silu(g) * u
        ys = lax.ragged_dot(act, w2, group_sizes)
        y = jnp.zeros((T * K, H), ys.dtype).at[sort_idx].set(ys)
        routed = jnp.sum(y.reshape(T, K, H) * topk_w[..., None].astype(ys.dtype), axis=1)
        shared = jax.nn.silu(flat @ sg) * (flat @ su) @ sd
        out = residual + (routed + shared).reshape(B, S, H)
        return out
    x = L0_attn_x
    x = x + _L0_attn_ref(_layernorm(x, axis=-1), L0_attn_w_attn, L0_attn_w_proj)
    x = x + _L0_ffn_ref(_layernorm(x, axis=-1), L0_ffn_norm_w, L0_ffn_router_w, L0_ffn_w1, L0_ffn_w2, L0_ffn_sg, L0_ffn_su, L0_ffn_sd)
    return x

_drawn_inputs = setup_inputs


def setup_inputs(seed=0):
    import zlib

    import numpy as np

    out = dict(_drawn_inputs(seed))
    spreads = {'L0_ffn_norm_w': (1.0, 0.2)}
    factors = {}
    for name, (base, spread) in spreads.items():
        noise = np.random.default_rng([zlib.crc32(name.encode()), seed]).standard_normal(out[name].shape)
        drawn = base * np.exp(spread * noise) if base else spread * noise
        out[name] = jnp.asarray(drawn.astype(out[name].dtype))
    for name, factor in factors.items():
        out[name] = (out[name] * factor).astype(out[name].dtype)
    return out
```

```python
from contextlib import ExitStack

import concourse.bass as bass
from concourse import mybir

F32 = mybir.dt.float32
F32R = mybir.dt.float32r
BF16 = mybir.dt.bfloat16
I32 = mybir.dt.int32
U32 = mybir.dt.uint32
ALU = mybir.AluOpType
ACT = mybir.ActivationFunctionType
X = mybir.AxisListType.X

P = 128
T, D = 1024, 256
TILES = T // P
DC = D // P
HEADS, HD = 16, 16
PAIRS = HEADS // 2
QK_SCALE = HD ** -0.5
STACK = 64
ROWS = 1 + 3 * HD
VW = HD + 1
EXPERTS, TOPK, INNER = 32, 4, 128
MAX_BLOCKS = (T * TOPK + EXPERTS * (P - 1)) // P
SLOTS = MAX_BLOCKS * P
RING = 4
P_RING = 3
EPS_LN, EPS_RMS = 1e-5, 1e-6
NEG = -1e30


def max_units():
    units, first, last = [], [], []
    halves = list(range(0, HEADS, 2)) + list(range(1, HEADS, 2))
    for i in range(TILES):
        first.append(len(units))
        width = (i + 1) * P
        w0 = min(width, 512)
        per = 512 // w0
        for a in range(0, HEADS, per):
            units.append((i, (halves if per > 1 else range(HEADS))[a:a + per], 0, w0, 0, width <= 512))
        if width > 512:
            w1 = width - 512
            per = 512 // w1
            for a in range(0, HEADS, per):
                units.append((i, (halves if per > 1 else range(HEADS))[a:a + per], 512, w1, 1, True))
        last.append(len(units) - 1)
    return units, first, last


def prob_units():
    units, first = [], []
    for i in range(TILES):
        first.append(len(units))
        for h in range(0, HEADS, 2):
            if i < 4:
                units.append((i, [h, h + 1]))
            else:
                units += [(i, [h]), (i, [h + 1])]
    return units, first


def layer(nc, x, w_attn, w_proj, norm_w, router_w, w1, w2, sg, su, sd, out):
    A_UNITS, A_FIRST, A_LAST = max_units()
    B_UNITS, B_FIRST = prob_units()
    NB = len(B_UNITS)
    STEPS = NB + 6
    MOE_STEPS = MAX_BLOCKS + 2

    a_at = [[] for _ in range(STEPS)]
    pe_at = [[] for _ in range(STEPS)]
    dve_at = [[] for _ in range(STEPS)]
    act_at = [[] for _ in range(STEPS)]
    pool_at = [[] for _ in range(STEPS)]
    for i in range(TILES - 2):
        n = B_FIRST[i + 1] - B_FIRST[i]
        todo = list(range(A_FIRST[i + 2], A_LAST[i + 2] + 1))
        for a, unit in enumerate(todo):
            a_at[B_FIRST[i] + a * n // len(todo)].append(unit)
    for i in range(TILES):
        s = B_FIRST[i + 1] if i + 1 < TILES else NB
        dve_at[s].append(("norm", i))
        pe_at[s].append(("y_turn", i))
        act_at[s + 1].append(("y_copy", i))
        pe_at[s + 1].append(("proj", i))
        dve_at[s + 2].append(("residual", i))
        pool_at[s + 2].append(("rstd", i))
        dve_at[s + 3].append(("h", i))
        pe_at[s + 3].append(("h_turn", i))
        act_at[s + 4].append(("h_copy", i))
        pe_at[s + 4].append(("logits", i))
        dve_at[s + 5].append(("top", i))
        if i:
            s = B_FIRST[i - 1]
            if i >= 4:
                dve_at[s + 1].append(("max_join", i))
            pe_at[s + 2].append(("max_turn", i))
            act_at[s + 3].append(("max_copy", i))

    order = [("max_turn", 0)] + [job for jobs in pe_at for job in jobs]
    turn = {job: n for n, job in enumerate(order)}

    ctx = ExitStack()
    with ctx:
        start = nc.sbuf_base + (-nc.sbuf_base) % 64
        end = nc.sbuf_usable_end
        cursor = [start]

        def sb(name, shape, dt, at=None):
            size = int(mybir.dt.size(dt))
            for n in shape[1:]:
                size *= n
            if at is None:
                at = cursor[0]
                cursor[0] += size + (-size) % 64
                assert cursor[0] <= end, (name, cursor[0], end)
            return nc.alloc_sbuf_tensor_at(name, shape, dt, offset=at)

        KB = 1024
        w1_at = cursor[0]
        w1_sb = sb("w1_sb", [P, EXPERTS * DC * D], F32)
        gathered = sb("gathered", [P, TILES * TOPK, D], F32, w1_at)
        q_at = cursor[0]
        q_stack = sb("q_stack", [P, PAIRS, T], F32R)
        w2_sb = sb("w2_sb", [P, EXPERTS * D], F32, q_at)
        k_at = cursor[0]
        k_stack = sb("k_stack", [P, PAIRS, T], F32R)
        shared_sig = sb("shared_sig", [P, 2, T], F32, k_at)
        shared_act = sb("shared_act", [P, 2, T], F32, k_at + 8 * KB)
        ys_sb = sb("ys_sb", [P, RING, D], F32, k_at)
        silu_sb = sb("silu_sb", [P, RING, P], F32, k_at + 4 * KB)
        xs_tok = sb("xs_tok", [P, RING, D], F32, k_at + 16 * KB)
        xs_feat = sb("xs_feat", [P, RING, DC, P], F32, k_at + 20 * KB)
        act_sb = sb("act_sb", [P, RING, P], F32, k_at + 24 * KB)
        act_feat = sb("act_feat", [P, RING, P], F32, k_at + 26 * KB)
        v_ext = sb("v_ext", [P, TILES, HEADS, VW], F32)
        x_sb = sb("x_sb", [P, TILES, D], F32)
        tok_at = cursor[0]
        xn = sb("xn", [P, TILES, D], F32)
        h_tok = sb("h_tok", [P, TILES, D], F32, tok_at)
        base = sb("base", [P, TILES, D], F32)
        feat_at = cursor[0]
        xn_feat = sb("xn_feat", [P, DC, T], F32)
        h_feat = sb("h_feat", [P, DC, T], F32, feat_at)
        st_at = cursor[0]
        q_tok = sb("q_tok", [P, 2, PAIRS, 2, STACK], F32)
        k_tok = sb("k_tok", [P, 2, PAIRS, 2, STACK], F32)
        probs = sb("probs", [P, P_RING, T], F32, st_at)
        onehot = sb("onehot", [P, TILES, TOPK, EXPERTS], F32, st_at)
        slot_of = sb("slot_of", [P, TILES, TOPK, EXPERTS], F32, st_at + 4 * KB)
        below = sb("below", [1, MAX_BLOCKS, EXPERTS], F32, st_at + 8 * KB)
        wa_at = cursor[0]
        wa_sb = sb("wa_sb", [P, DC, 3 * D], F32)
        wp_sb = sb("wp_sb", [P, DC, D], F32)
        sg_sb = sb("sg_sb", [P, DC, D], F32)
        su_sb = sb("su_sb", [P, DC, D], F32)
        sd_sb = sb("sd_sb", [P, DC, D], F32)
        nw_sb = sb("nw_sb", [P, D], F32)
        zeros = sb("zeros", [P, D], F32)
        ident = sb("ident", [P, P], F32)
        ident_b = sb("ident_b", [P, P], BF16)
        before_b = sb("before_b", [P, P], BF16)
        ones_b = sb("ones_b", [P, P], BF16)
        future_b = sb("future_b", [P, P], BF16)
        router_sb = sb("router_sb", [EXPERTS, D], F32)
        router_feat = sb("router_feat", [P, DC, EXPERTS], F32)
        powers = sb("powers", [P, 16], F32)
        iota_e = sb("iota_e", [P, EXPERTS], F32)
        iota_b = sb("iota_b", [1, MAX_BLOCKS], F32)
        stats = sb("stats", [P, TILES, 6], F32)
        mean_var = sb("mean_var", [P, TILES, 2], F32)
        var_eps = sb("var_eps", [P, TILES], F32)
        rstd = sb("rstd", [P, TILES], F32)
        row_max = sb("row_max", [P, 2, TILES, HEADS], F32)
        neg_max = sb("neg_max", [HEADS, 2, P], F32R)
        denom = sb("denom", [P, HEADS], F32)
        y_tok = sb("y_tok", [P, D], F32, st_at + 12 * KB)
        y_feat = sb("y_feat", [P, DC, P], F32, st_at + 13 * KB)
        stats2 = sb("stats2", [P, 6], F32)
        mean_var2 = sb("mean_var2", [P, 2, 2], F32)
        var_args = sb("var_args", [P, 2, 2], F32)
        rstd2 = sb("rstd2", [P, 2, 2], F32)
        h_raw = sb("h_raw", [P, D], F32, st_at + 14 * KB)
        ln2 = sb("ln2", [P, D], F32, st_at + 15 * KB)
        logit_sb = sb("logit_sb", [P, TILES, EXPERTS], F32, wa_at)
        top_v = sb("top_v", [P, TILES, 8], F32, wa_at + 2 * KB)
        top_i = sb("top_i", [P, TILES, 8], U32, wa_at + 3 * KB)
        top_d = sb("top_d", [P, TILES, TOPK], F32)
        top_e = sb("top_e", [P, TILES, TOPK], F32)
        top_sum = sb("top_sum", [P, TILES], F32)
        top_w = sb("top_w", [P, TILES, TOPK], F32)
        idx_f = sb("idx_f", [P, TILES, TOPK], F32, wa_at + 5 * KB)
        chosen = sb("chosen", [P, TILES, EXPERTS], BF16, wa_at + 4 * KB)
        count_i = sb("count_i", [P, 2, EXPERTS], I32, wa_at + 5 * KB + 128)
        nblk = sb("nblk", [P, EXPERTS], F32)
        nblk_end = sb("nblk_end", [P, EXPERTS], F32)
        nblk_start = sb("nblk_start", [P, EXPERTS], F32)
        slot_te = sb("slot_te", [P, TILES, EXPERTS], F32, wa_at + KB)
        slot_f = sb("slot_f", [P, TILES * TOPK], F32, wa_at + 5 * KB + 384)
        slot_i = sb("slot_i", [P, TILES * TOPK], I32)
        expert_f = sb("expert_f", [1, MAX_BLOCKS], F32, wa_at + 5 * KB + 512)
        w1_off = sb("w1_off", [1, MAX_BLOCKS], I32)
        w2_off = sb("w2_off", [1, MAX_BLOCKS], I32)

        xs_dram = nc.dram_tensor("xs_dram", [SLOTS, D], F32).ap()
        ys_dram = nc.dram_tensor("ys_dram", [SLOTS, D], F32).ap()

        ps = ctx.enter_context(nc.psum_tensor("ps", [P, 8, 512], F32))

        def sem(name):
            return ctx.enter_context(nc.semaphore(name))

        x_loaded = [sem(f"x_loaded{n}") for n in range(4)]
        wa_loaded, wp_loaded, router_loaded = sem("wa_loaded"), sem("wp_loaded"), sem("router_loaded")
        nw_loaded, shared_loaded = sem("nw_loaded"), sem("shared_loaded")
        w1_loaded, w2_loaded, xs_cleared = sem("w1_loaded"), sem("w2_loaded"), sem("xs_cleared")
        zeros_ready, consts, stack_consts = sem("zeros_ready"), sem("consts"), sem("stack_consts")
        pool_step, dve_step = sem("pool_step"), sem("dve_step")
        stats_ready, rstd_ready, xn_ready = sem("stats_ready"), sem("rstd_ready"), sem("xn_ready")
        router_turned, router_ready = sem("router_turned"), sem("router_ready")
        xn_turned, xn_feat_ready = sem("xn_turned"), sem("xn_feat_ready")
        qk_made, v_made = sem("qk_made"), sem("v_made")
        high_ready, low_ready, v_ready = sem("high_ready"), sem("low_ready"), sem("v_ready")
        stacked = [sem("stacked0"), sem("stacked1")]
        stack_ready = [sem("stack_ready_act"), sem("stack_ready_dve")]
        rows_scored, row_maxed, max_joined = sem("rows_scored"), sem("row_maxed"), sem("max_joined")
        max_placed = [sem("max_placed0"), sem("max_placed1")]
        scored, exped, masked, summed = sem("scored"), sem("exped"), sem("masked"), sem("summed")
        y_ready, misc_made, misc_used = sem("y_ready"), sem("misc_made"), sem("misc_used")
        var_ready, rstd2_ready, h_ready = sem("var_ready"), sem("rstd2_ready"), sem("h_ready")
        base_ready, top_ready, top_exped = sem("base_ready"), sem("top_ready"), sem("top_exped")
        chosen_ready, ranked, slots_ready = sem("chosen_ready"), sem("ranked"), sem("slots_ready")
        offsets_ready = sem("offsets_ready")
        shared_up, shared_silu, shared_ready = sem("shared_up"), sem("shared_silu"), sem("shared_ready")
        shared_down, shared_added = sem("shared_down"), sem("shared_added")
        scattered = sem("scattered")
        xs_loaded = [sem(f"xs_loaded{r}") for r in range(RING)]
        ys_stored = [sem(f"ys_stored{r}") for r in range(RING)]
        xs_turned, xs_ready, gate_up = sem("xs_turned"), sem("xs_ready"), sem("gate_up")
        silu_ready, act_ready, act_turned = sem("silu_ready"), sem("act_ready"), sem("act_turned")
        act_feat_ready, down, ys_ready = sem("act_feat_ready"), sem("down"), sem("ys_ready")
        row_gathered = [sem(f"row_gathered{t}") for t in range(TILES)]
        combined, stored = sem("combined"), sem("stored")

        x_d = x.rearrange("a (t p) d -> p (a t) d", p=P)
        out_d = out.rearrange("a (t p) d -> p (a t) d", p=P)

        def head_rows(h):
            return 64 * (h % 2), 64 * (h % 2) + ROWS, h // 2

        def over_blocks(engine, step):
            head = 2 * RING - 1
            turns = (MAX_BLOCKS - RING - head) // RING
            for b in range(head):
                step(b, b, b % RING, b // RING)
            with engine.Fori(0, turns) as it:
                for n in range(head, head + RING):
                    step(it * RING + n, n, n % RING, it + n // RING)
            for b in range(head + turns * RING, MAX_BLOCKS + 2):
                step(b, b, b % RING, b // RING)

        block = ctx.enter_context(nc.Block())

        @block.sync
        def _(sp):
            for n in range(4):
                sp.dma_start(x_sb[:, 2 * n:2 * n + 2, :], x_d[:, 2 * n:2 * n + 2, :]).then_inc(x_loaded[n], 16)
            sp.dma_start(router_sb[:, :], router_w).then_inc(router_loaded, 16)
            sp.dma_start(wa_sb[:, :, :], w_attn.rearrange("(c p) n -> p c n", p=P)).then_inc(wa_loaded, 16)
            sp.dma_start(wp_sb[:, :, :], w_proj.rearrange("(c p) n -> p c n", p=P)).then_inc(wp_loaded, 16)
            sp.dma_start(nw_sb[:, :], norm_w.rearrange("(a n) -> a n", a=1).broadcast_to([P, D])).then_inc(nw_loaded, 16)
            for dst, src in ((sg_sb, sg), (su_sb, su), (sd_sb, sd)):
                sp.dma_start(dst[:, :, :], src.rearrange("(c p) n -> p c n", p=P)).then_inc(shared_loaded, 16)
            sp.wait_ge(zeros_ready, 1)
            sp.dma_start(xs_dram.rearrange("(b p) d -> p b d", p=P),
                         zeros[:, :].unsqueeze(1).broadcast_to([P, MAX_BLOCKS, D])).then_inc(xs_cleared, 16)
            w1_v = w1_sb[:, :].rearrange("p (e c n) -> p e c n", e=EXPERTS, c=DC)
            for c in range(DC):
                sp.dma_start(w1_v[:, :, c, :], w1[:, c * P:(c + 1) * P, :].rearrange("e p n -> p e n")).then_inc(w1_loaded, 16)
            for i in range(TILES):
                sp.wait_ge(misc_used, turn["max_turn", i] + 1)
                sp.wait_ge(rows_scored, A_LAST[i] + 1)
                for half in range(2):
                    sp.dma_start(q_stack[64 * half:64 * half + 1, :, i * P:(i + 1) * P].bitcast(F32),
                                 neg_max[half:HEADS:2, i % 2, :].bitcast(F32)).then_inc(max_placed[i % 2], 16)
            sp.wait_ge(summed, NB)
            sp.dma_start(w2_sb[:, :].rearrange("p (e n) -> p e n", e=EXPERTS),
                         w2.rearrange("e p n -> p e n")).then_inc(w2_loaded, 16)

            def load(b, r):
                sp.dma_start(xs_tok[:, r, :], xs_dram[bass.ts(b, P), :]).then_inc(xs_loaded[r], 16)

            sp.wait_ge(scattered, 16 * TILES * TOPK)
            for b in range(RING):
                load(b, b)

            def step(b, n, r, q):
                if n + RING < MAX_BLOCKS:
                    sp.wait_ge(xs_turned, b + 1)
                    load(b + RING, r)
                if n >= 2:
                    r2 = (r - 2) % RING
                    sp.wait_ge(ys_ready, b - 1)
                    sp.dma_start(ys_dram[bass.ts(b - 2, P), :], ys_sb[:, r2, :]).then_inc(ys_stored[r2], 16)

            over_blocks(sp, step)
            for t in range(TILES):
                sp.wait_ge(combined, t + 1)
                sp.dma_start(out_d[:, t, :], base[:, t, :]).then_inc(stored, 16)
            sp.wait_ge(stored, 16 * TILES)

        @block.gpsimd
        def _(pool):
            steps = [0]

            def link(ins):
                steps[0] += 1
                ins.then_inc(pool_step, 1)
                pool.wait_ge(pool_step, steps[0])

            pool.memset(zeros[:, :], 0.0).then_inc(zeros_ready, 1)
            pool.memset(powers[:, :], -0.5)
            pool.memset(ones_b[:, :], 1.0)
            link(pool.memset(ident[:, :], 0.0))
            link(pool.affine_select(out=ident[:, :], in_=ident[:, :], compare_op=ALU.not_equal, fill=1.0, base=0,
                                    pattern=[[-1, P]], channel_multiplier=1))
            pool.tensor_copy(ident_b[:, :], ident[:, :])
            link(pool.memset(future_b[:, :], 0.0))
            pool.affine_select(out=future_b[:, :], in_=future_b[:, :], compare_op=ALU.is_ge, fill=NEG, base=0,
                               pattern=[[-1, P]], channel_multiplier=1)
            pool.affine_select(out=before_b[:, :], in_=ones_b[:, :], compare_op=ALU.is_gt, fill=0.0, base=0,
                               pattern=[[1, P]], channel_multiplier=-1)
            pool.iota(iota_e[:, :], [[1, EXPERTS]], base=0, channel_multiplier=0, allow_small_or_imprecise_dtypes=True)
            link(pool.iota(iota_b[:, :], [[1, MAX_BLOCKS]], base=0, channel_multiplier=0,
                           allow_small_or_imprecise_dtypes=True))
            pool.memset(v_ext[:, :, :, HD:VW], 1.0).then_inc(consts, 1)
            for g in range(2):
                pool.wait_ge(stats_ready, g + 1)
                pool.tensor_tensor(rstd[:, 4 * g:4 * g + 4], var_eps[:, 4 * g:4 * g + 4], powers[:, 0:4],
                                   ALU.pow).then_inc(rstd_ready, 1)

            def mask(u):
                i, heads = B_UNITS[u]
                pool.wait_ge(exped, u + 1)
                v = probs[:, u % P_RING, :].rearrange("p (a q) -> p a q", a=2 if len(heads) == 2 else 1)
                v = v[:, :, i * P:(i + 1) * P]
                pool.affine_select(out=v, in_=v, compare_op=ALU.is_ge, fill=0.0, base=0,
                                   pattern=[[0, len(heads)], [1, P]], channel_multiplier=-1).then_inc(masked, 1)

            for u in range(STEPS):
                if u < NB:
                    mask(u)
                for _, i in pool_at[u]:
                    pool.wait_ge(var_ready, i + 1)
                    pool.tensor_tensor(rstd2[:, i % 2, :], var_args[:, i % 2, :], powers[:, 0:2],
                                       ALU.pow).then_inc(rstd2_ready, 1)
                    pool.wait_ge(rstd2_ready, i + 1)
                    link(pool.tensor_scalar(ln2[:, :], x_sb[:, i, :], mean_var2[:, i % 2, 0:1], rstd2[:, i % 2, 0:1],
                                            ALU.subtract, ALU.mult))
                    pool.tensor_tensor(base[:, i, :], x_sb[:, i, :], ln2[:, :], ALU.add).then_inc(base_ready, 1)
                    if i + 1 < TILES:
                        pool.wait_ge(base_ready, i + 1)

            pool.wait_ge(slots_ready, 1)
            pool.wait_ge(xs_cleared, 16)
            for n in range(TILES * TOPK):
                pool.indirect_dma_start(xs_dram, bass.IndirectOffsetOnAxis(slot_i[:, n:n + 1], 0),
                                        h_tok[:, n // TOPK, :], None).then_inc(scattered, 16)
            for r in range(RING):
                pool.wait_ge(ys_stored[r], 16 * len(range(r, MAX_BLOCKS, RING)))
            for n in range(TILES * TOPK):
                pool.indirect_dma_start(gathered[:, n, :], None, ys_dram,
                                        bass.IndirectOffsetOnAxis(slot_i[:, n:n + 1], 0)).then_inc(row_gathered[n // TOPK], 16)

        @block.tensor
        def _(pe):
            pe.wait_ge(consts, 1)
            pe.wait_ge(router_loaded, 16)
            for c in range(DC):
                last = pe.transpose(ps[:, 7, c * EXPERTS:(c + 1) * EXPERTS], router_sb[:, c * P:(c + 1) * P],
                                    ident[0:EXPERTS, 0:EXPERTS])
            last.then_inc(router_turned, 1)

            def turn_xn(j):
                pe.wait_ge(xn_ready, j + 1)
                if j >= 2:
                    pe.wait_ge(xn_feat_ready, j - 1)
                for c in range(DC):
                    last = pe.transpose(ps[:, j % 2, c * P:(c + 1) * P], xn[:, j, c * P:(c + 1) * P], ident[:, :])
                last.then_inc(xn_turned, 1)

            def project(j):
                pe.wait_ge(xn_feat_ready, j + 1)
                if j >= 2:
                    pe.wait_ge(low_ready, 2 * (j - 1))
                    pe.wait_ge(v_ready, j - 1)
                for c in range(DC):
                    last = pe.matmul(ps[:, 2 + j % 2, :], xn_feat[:, c, j * P:(j + 1) * P], wa_sb[:, c, 0:2 * D],
                                     start=(c == 0), stop=(c == DC - 1))
                last.then_inc(qk_made, 1)
                for c in range(DC):
                    last = pe.matmul(ps[:, 4 + j % 2, 0:D], xn_feat[:, c, j * P:(j + 1) * P], wa_sb[:, c, 2 * D:3 * D],
                                     start=(c == 0), stop=(c == DC - 1))
                last.then_inc(v_made, 1)

            def stack(j):
                pe.wait_ge(high_ready, 4 * (j + 1))
                pe.wait_ge(low_ready, 2 * (j + 1))
                for g in range(4):
                    src = (q_tok, k_tok)[g // 2]
                    n = 2 * j + g // 2
                    if n:
                        pe.wait_ge(stack_ready[g % 2], n)
                    for p in range(4):
                        pair = 4 * (g % 2) + p
                        last = pe.transpose(ps[:, 6 + g % 2, p * P:(p + 1) * P],
                                            src[:, j % 2, pair, :, :].rearrange("p a c -> p (a c)"), ident[:, :])
                    last.then_inc(stacked[g % 2], 1)

            turn_xn(0)
            pe.wait_ge(wa_loaded, 16)
            pe.wait_ge(router_ready, 1)
            for j in range(TILES):
                if j + 1 < TILES:
                    turn_xn(j + 1)
                project(j)
                if j:
                    stack(j - 1)
            stack(TILES - 1)

            pe.wait_ge(xn_feat_ready, TILES)
            pe.wait_ge(v_ready, TILES)
            for g in range(2):
                pe.wait_ge(stack_ready[g], 2 * TILES)

            def score_rows(a):
                i, heads, k0, kw, part, diagonal = A_UNITS[a]
                if a >= 2:
                    pe.wait_ge(row_maxed, a - 1)
                for n, h in enumerate(heads):
                    r0, r1, pair = head_rows(h)
                    last = pe.matmul(ps[:, a % 2, n * kw:(n + 1) * kw], q_stack[r0:r1, pair, i * P:(i + 1) * P],
                                     k_stack[r0:r1, pair, k0:k0 + kw], start=True, stop=not diagonal)
                    if diagonal:
                        last = pe.matmul(ps[:, a % 2, (n + 1) * kw - P:(n + 1) * kw], ident_b[:, :], future_b[:, :],
                                         start=False, stop=True)
                last.then_inc(rows_scored, 1)

            def turn_max(i):
                if i >= 4:
                    pe.wait_ge(max_joined, i - 3)
                else:
                    pe.wait_ge(row_maxed, A_LAST[i] + 1)
                return pe.transpose(ps[0:HEADS, 7, 0:P], row_max[:, 0, i, :], ident[:, :])

            def score_keys(u):
                i, heads = B_UNITS[u]
                if u >= 2:
                    pe.wait_ge(exped, u - 1)
                if u == B_FIRST[i]:
                    pe.wait_ge(max_placed[i % 2], 32 * (i // 2 + 1))
                bank = 2 + 2 * (u % 2)
                for jt in range(i + 1):
                    for n, h in enumerate(heads):
                        r0, r1, pair = head_rows(h)
                        at = 512 * n + jt * P
                        last = pe.matmul(ps[:, bank + at // 512, at % 512:at % 512 + P],
                                         k_stack[r0:r1, pair, jt * P:(jt + 1) * P],
                                         q_stack[r0:r1, pair, i * P:(i + 1) * P], start=True, stop=True)
                last.then_inc(scored, 1)

            def sum_values(u):
                i, heads = B_UNITS[u]
                pe.wait_ge(masked, u + 1)
                if u == B_FIRST[i] and i:
                    pe.wait_ge(y_ready, i)
                for n, h in enumerate(heads):
                    for jt in range(i + 1):
                        at = 512 * n + jt * P
                        last = pe.matmul(ps[:, 6, h * VW:(h + 1) * VW], probs[:, u % P_RING, at:at + P],
                                         v_ext[:, jt, h, :], start=(jt == 0), stop=(jt == i))
                last.then_inc(summed, 1)

            def job(what, i):
                if turn[what, i]:
                    pe.wait_ge(misc_used, turn[what, i])
                if what == "max_turn":
                    last = turn_max(i)
                elif what == "y_turn":
                    pe.wait_ge(y_ready, i + 1)
                    for c in range(DC):
                        last = pe.transpose(ps[:, 7, c * P:(c + 1) * P], y_tok[:, c * P:(c + 1) * P], ident[:, :])
                elif what == "proj":
                    pe.wait_ge(wp_loaded, 16)
                    for c in range(DC):
                        last = pe.matmul(ps[:, 7, D:2 * D], y_feat[:, c, :], wp_sb[:, c, :],
                                         start=(c == 0), stop=(c == DC - 1))
                elif what == "h_turn":
                    pe.wait_ge(h_ready, i + 1)
                    for c in range(DC):
                        last = pe.transpose(ps[:, 7, c * P:(c + 1) * P], h_tok[:, i, c * P:(c + 1) * P], ident[:, :])
                elif what == "logits":
                    for c in range(DC):
                        last = pe.matmul(ps[:, 7, D:D + EXPERTS], h_feat[:, c, i * P:(i + 1) * P], router_feat[:, c, :],
                                         start=(c == 0), stop=(c == DC - 1))
                last.then_inc(misc_made, 1)

            for a in range(A_LAST[0] + 1):
                score_rows(a)
            job("max_turn", 0)
            for a in range(A_FIRST[1], A_LAST[1] + 1):
                score_rows(a)
            score_keys(0)
            for u in range(STEPS):
                if u + 1 < NB:
                    score_keys(u + 1)
                for a in a_at[u]:
                    score_rows(a)
                if u < NB:
                    sum_values(u)
                for what, i in pe_at[u]:
                    job(what, i)

            pe.wait_ge(shared_loaded, 48)
            pe.wait_ge(row_maxed, len(A_UNITS))
            pe.wait_ge(exped, NB)
            pe.wait_ge(misc_used, len(order))

            def up(n):
                chunk, inner = n // 2, n % 2
                bank = 2 * (n % 3)
                if n >= 3:
                    pe.wait_ge(shared_ready, n - 2)
                for w, b in ((sg_sb, bank), (su_sb, bank + 1)):
                    for c in range(DC):
                        last = pe.matmul(ps[:, b, :], w[:, c, inner * P:(inner + 1) * P],
                                         h_feat[:, c, chunk * 512:(chunk + 1) * 512], start=(c == 0), stop=(c == DC - 1))
                last.then_inc(shared_up, 1)

            up(0)
            pe.wait_ge(chosen_ready, 1)
            ranks = ps[:, 6, 0:TILES * EXPERTS].rearrange("p (t e) -> p t e", t=TILES)
            pe.matmul(ranks, before_b[:, :], chosen[:, :, :], start=True, stop=False)
            for t in range(TILES - 1):
                n = TILES - 1 - t
                pe.matmul(ranks[:, t + 1:, :], ones_b[:, :], chosen[:, t:t + 1, :].broadcast_to([P, n, EXPERTS]),
                          start=False, stop=(t == TILES - 2))
            for t in range(TILES):
                last = pe.matmul(ps[:, 6, 256:256 + EXPERTS], ones_b[:, :], chosen[:, t, :],
                                 start=(t == 0), stop=(t == TILES - 1))
            last.then_inc(ranked, 1)
            for n in range(1, 4):
                up(n)
            pe.wait_ge(slots_ready, 1)
            for t in range(TILES):
                if t % 4 == 0:
                    pe.wait_ge(shared_ready, 2 * (t // 4) + 2)
                if t >= 2:
                    pe.wait_ge(shared_added, t - 1)
                for c in range(2):
                    last = pe.matmul(ps[:, 6 + t % 2, 0:D], shared_act[:, c, t * P:(t + 1) * P],
                                     sd_sb[:, c, :], start=(c == 0), stop=(c == 1))
                last.then_inc(shared_down, 1)

            pe.wait_ge(w1_loaded, 16 * DC)
            pe.wait_ge(w2_loaded, 16)
            pe.wait_ge(offsets_ready, 1)
            pe.wait_ge(shared_ready, 4)

            def turn_x(b, n, r, q):
                pe.wait_ge(xs_loaded[r], 16 * q + 16)
                for c in range(DC):
                    last = pe.transpose(ps[:, 2 + n % 2, c * P:(c + 1) * P], xs_tok[:, r, c * P:(c + 1) * P], ident[:, :])
                last.then_inc(xs_turned, 1)

            def step(b, n, r, q):
                if n < MAX_BLOCKS:
                    pe.wait_ge(xs_ready, b + 1)
                    if n >= 2:
                        pe.wait_ge(act_ready, b - 1)
                    at = pe.value_load(w1_off[0:1, bass.ds(b, 1)], min_val=0, max_val=(EXPERTS - 1) * DC * D)
                    for c in range(DC):
                        last = pe.matmul(ps[:, n % 2, 0:D], xs_feat[:, r, c, :], w1_sb[:, bass.ds(at + c * D, D)],
                                         start=(c == 0), stop=(c == DC - 1))
                    last.then_inc(gate_up, 1)
                if 1 <= n <= MAX_BLOCKS:
                    pe.wait_ge(act_ready, b)
                    if n >= 3:
                        pe.wait_ge(act_feat_ready, b - 2)
                    pe.transpose(ps[:, 4 + (n - 1) % 2, 0:P], act_sb[:, (r - 1) % RING, :], ident[:, :]).then_inc(act_turned, 1)
                if n + 1 < MAX_BLOCKS:
                    if n >= 1:
                        pe.wait_ge(xs_ready, b)
                    turn_x(b + 1, n + 1, (r + 1) % RING, q + int(r == RING - 1))
                if n >= 2:
                    pe.wait_ge(act_feat_ready, b - 1)
                    if n >= 4:
                        pe.wait_ge(ys_ready, b - 3)
                    at = pe.value_load(w2_off[0:1, bass.ds(b - 2, 1)], min_val=0, max_val=(EXPERTS - 1) * D)
                    pe.matmul(ps[:, 6 + n % 2, 0:D], act_feat[:, (r - 2) % RING, :], w2_sb[:, bass.ds(at, D)],
                              start=True, stop=True).then_inc(down, 1)

            turn_x(0, 0, 0, 0)
            over_blocks(pe, step)

        @block.scalar
        def _(act):
            act.wait_ge(router_turned, 1)
            act.activation(router_feat[:, :, :].rearrange("p c e -> p (c e)"), ps[:, 7, 0:DC * EXPERTS],
                           ACT.Copy).then_inc(router_ready, 1)
            for j in range(TILES + 1):
                if j < TILES:
                    act.wait_ge(xn_turned, j + 1)
                    act.activation(xn_feat[:, :, j * P:(j + 1) * P],
                                   ps[:, j % 2, 0:D].rearrange("p (c q) -> p c q", c=DC), ACT.Copy).then_inc(xn_feat_ready, 1)
                    act.wait_ge(qk_made, j + 1)
                    if j == 0:
                        act.wait_ge(stack_consts, 1)
                    if j >= 2:
                        act.wait_ge(stacked[1], 2 * (j - 1))
                    for dst, at, cols, scale in ((q_tok, 0, (1, 1 + 2 * HD), QK_SCALE), (k_tok, D, (1, 1 + HD), 1.0)):
                        for col in cols:
                            act.activation(
                                dst[:, j % 2, :, :, col:col + HD].rearrange("p a b d -> p (a b) d").bitcast(F32R),
                                ps[:, 2 + j % 2, at:at + D].rearrange("p (h d) -> p h d", h=HEADS),
                                ACT.Copy, scale=scale).then_inc(high_ready, 1)
                if j:
                    for g, dst in enumerate((q_stack, k_stack)):
                        act.wait_ge(stacked[0], 2 * (j - 1) + g + 1)
                        act.activation(dst[:, 0:4, (j - 1) * P:j * P], ps[:, 6, :].rearrange("p (a q) -> p a q", a=4),
                                       ACT.Copy).then_inc(stack_ready[0], 1)

            def exp(u):
                i, heads = B_UNITS[u]
                act.wait_ge(scored, u + 1)
                if u >= P_RING:
                    act.wait_ge(summed, u - P_RING + 1)
                bank = 2 + 2 * (u % 2)
                if len(heads) == 2:
                    n = (i + 1) * P
                    act.activation(probs[:, u % P_RING, :].rearrange("p (a q) -> p a q", a=2)[:, :, 0:n],
                                   ps[:, bank:bank + 2, 0:n], ACT.Exp).then_inc(exped, 1)
                else:
                    n = (i + 1) * P
                    act.activation(probs[:, u % P_RING, 0:n],
                                   ps[:, bank:bank + 2, :].rearrange("p a q -> p (a q)")[:, 0:n], ACT.Exp).then_inc(exped, 1)

            def job(what, i):
                act.wait_ge(misc_made, turn[what.replace("copy", "turn"), i] + 1)
                if what == "max_copy":
                    if i >= 2:
                        act.wait_ge(max_placed[i % 2], 32 * (i // 2))
                    act.activation(neg_max[:, i % 2, :], ps[0:HEADS, 7, 0:P], ACT.Copy, scale=-1.0).then_inc(misc_used, 1)
                    return
                dst = y_feat[:, :, :] if what == "y_copy" else h_feat[:, :, i * P:(i + 1) * P]
                act.activation(dst, ps[:, 7, 0:D].rearrange("p (c q) -> p c q", c=DC), ACT.Copy).then_inc(misc_used, 1)

            job("max_copy", 0)
            for u in range(STEPS):
                if u < NB:
                    exp(u)
                for what, i in act_at[u]:
                    job(what, i)
            act.wait_ge(top_ready, TILES)
            act.activation(top_e[:, :, :], top_d[:, :, :], ACT.Exp).then_inc(top_exped, 1)
            act.wait_ge(summed, NB)
            for n in range(4):
                chunk, inner = n // 2, n % 2
                act.wait_ge(shared_up, n + 1)
                act.activation(shared_sig[:, inner, chunk * 512:(chunk + 1) * 512], ps[:, 2 * (n % 3), :],
                               ACT.Silu).then_inc(shared_silu, 1)

            def step(b, n, r, q):
                if n < MAX_BLOCKS:
                    act.wait_ge(gate_up, b + 1)
                    act.activation(silu_sb[:, r, :], ps[:, n % 2, 0:P], ACT.Silu).then_inc(silu_ready, 1)
                if n >= 2:
                    r2 = (r - 2) % RING
                    act.wait_ge(down, b - 1)
                    if n - 2 >= RING:
                        act.wait_ge(ys_stored[r2], 16 * (q if r >= 2 else q - 1))
                    act.activation(ys_sb[:, r2, :], ps[:, 6 + n % 2, 0:D], ACT.Copy).then_inc(ys_ready, 1)

            over_blocks(act, step)

        @block.vector
        def _(dve):
            steps = [0]

            def link(ins):
                steps[0] += 1
                ins.then_inc(dve_step, 1)
                dve.wait_ge(dve_step, steps[0])

            def note(ins):
                steps[0] += 1
                ins.then_inc(dve_step, 1)

            note(dve.memset(q_tok[:, :, :, :, :], 0.0))
            note(dve.memset(k_tok[:, :, :, :, :], 0.0))
            dve.wait_ge(dve_step, steps[0])
            dve.memset(k_tok[:, :, :, :, 0:1], 1.0).then_inc(stack_consts, 1)
            for g in range(2):
                for j in range(4 * g, 4 * g + 4):
                    dve.wait_ge(x_loaded[j // 2], 16)
                    note(dve.bn_stats(stats[:, j, :], x_sb[:, j, :]))
                dve.wait_ge(dve_step, steps[0])
                for j in range(4 * g, 4 * g + 4):
                    note(dve.bn_aggr(mean_var[:, j, :], stats[:, j, :]))
                dve.wait_ge(dve_step, steps[0])
                dve.tensor_scalar(var_eps[:, 4 * g:4 * g + 4], mean_var[:, 4 * g:4 * g + 4, 1], EPS_LN, None,
                                  ALU.add).then_inc(stats_ready, 1)

            def normalise(j):
                dve.wait_ge(rstd_ready, j // 4 + 1)
                dve.tensor_scalar(xn[:, j, :], x_sb[:, j, :], mean_var[:, j, 0:1], rstd[:, j:j + 1],
                                  ALU.subtract, ALU.mult).then_inc(xn_ready, 1)

            normalise(0)
            normalise(1)
            for j in range(TILES + 1):
                if j + 2 < TILES:
                    normalise(j + 2)
                if j:
                    for g, dst in enumerate((q_stack, k_stack)):
                        dve.wait_ge(stacked[1], 2 * (j - 1) + g + 1)
                        dve.tensor_copy(dst[:, 4:8, (j - 1) * P:j * P],
                                        ps[:, 7, :].rearrange("p (a q) -> p a q", a=4)).then_inc(stack_ready[1], 1)
                if j < TILES:
                    dve.wait_ge(v_made, j + 1)
                    if j == 0:
                        dve.wait_ge(consts, 1)
                    dve.tensor_copy(v_ext[:, j, :, 0:HD],
                                    ps[:, 4 + j % 2, 0:D].rearrange("p (h d) -> p h d", h=HEADS)).then_inc(v_ready, 1)
                    for n, (dst, at, low, scale) in enumerate(((q_tok, 0, 1 + HD, QK_SCALE), (k_tok, D, 1 + 2 * HD, 1.0))):
                        dve.wait_ge(high_ready, 4 * (j + 1))
                        dve.scalar_tensor_tensor(
                            out=dst[:, j % 2, :, :, low:low + HD].rearrange("p a b d -> p (a b) d"),
                            in0=ps[:, 2 + j % 2, at:at + D].rearrange("p (h d) -> p h d", h=HEADS),
                            scalar=scale,
                            in1=dst[:, j % 2, :, :, 1:1 + HD].rearrange("p a b d -> p (a b) d"),
                            op0=ALU.mult, op1=ALU.subtract).then_inc(low_ready, 1)

            def maximum(a):
                i, heads, k0, kw, part, _ = A_UNITS[a]
                dve.wait_ge(rows_scored, a + 1)
                dve.tensor_reduce(row_max[:, part, i, heads[0]:heads[-1] + 1:2 if len(heads) > 1 else 1],
                                  ps[:, a % 2, 0:len(heads) * kw].rearrange("p (h k) -> p h k", h=len(heads)),
                                  X, ALU.max).then_inc(row_maxed, 1)

            def job(what, i):
                if what == "max_join":
                    dve.wait_ge(row_maxed, A_LAST[i] + 1)
                    dve.tensor_tensor(row_max[:, 0, i, :], row_max[:, 0, i, :], row_max[:, 1, i, :],
                                      ALU.max).then_inc(max_joined, 1)
                elif what == "norm":
                    dve.wait_ge(summed, B_FIRST[i + 1] if i + 1 < TILES else NB)
                    sums = ps[:, 6, 0:HEADS * VW].rearrange("p (h c) -> p h c", h=HEADS)
                    if i:
                        dve.wait_ge(misc_made, turn["y_turn", i - 1] + 1)
                    link(dve.reciprocal(denom[:, :], sums[:, :, HD]))
                    dve.tensor_tensor(y_tok[:, :].rearrange("p (h d) -> p h d", h=HEADS), sums[:, :, 0:HD],
                                      denom[:, :].unsqueeze(2).broadcast_to([P, HEADS, HD]), ALU.mult).then_inc(y_ready, 1)
                elif what == "residual":
                    dve.wait_ge(misc_made, turn["proj", i] + 1)
                    x_i = x_sb[:, i, :]
                    ins = dve.tensor_tensor(x_i, x_i, ps[:, 7, D:2 * D], ALU.add)
                    ins.then_inc(misc_used, 1)
                    dve.wait_ge(misc_used, turn["proj", i] + 1)
                    link(dve.bn_stats(stats2[:, :], x_i))
                    if i >= 2:
                        dve.wait_ge(base_ready, i - 1)
                    link(dve.bn_aggr(mean_var2[:, i % 2, :], stats2[:, :]))
                    var = mean_var2[:, i % 2, 1:2]
                    link(dve.tensor_scalar(var_args[:, i % 2, 0:1], var, EPS_LN, None, ALU.add))
                    dve.scalar_tensor_tensor(out=var_args[:, i % 2, 1:2], in0=var_args[:, i % 2, 0:1], scalar=EPS_RMS,
                                             in1=var, op0=ALU.mult, op1=ALU.add).then_inc(var_ready, 1)
                elif what == "h":
                    dve.wait_ge(rstd2_ready, i + 1)
                    link(dve.tensor_scalar(h_raw[:, :], x_sb[:, i, :], mean_var2[:, i % 2, 0:1], rstd2[:, i % 2, 1:2],
                                           ALU.subtract, ALU.mult))
                    if i == 0:
                        dve.wait_ge(nw_loaded, 16)
                    dve.tensor_tensor(h_tok[:, i, :], h_raw[:, :], nw_sb[:, :], ALU.mult).then_inc(h_ready, 1)
                    dve.wait_ge(h_ready, i + 1)
                elif what == "top":
                    dve.wait_ge(misc_made, turn["logits", i] + 1)
                    dve.tensor_copy(logit_sb[:, i, :], ps[:, 7, D:D + EXPERTS]).then_inc(misc_used, 1)
                    dve.wait_ge(misc_used, turn["logits", i] + 1)
                    link(dve.max(top_v[:, i, :], logit_sb[:, i, :]))
                    note(dve.max_index(top_i[:, i, :], top_v[:, i, :], logit_sb[:, i, :]))
                    dve.tensor_scalar(top_d[:, i, :], top_v[:, i, 0:TOPK], top_v[:, i, 0:1], None,
                                      ALU.subtract).then_inc(top_ready, 1)

            for a in range(A_LAST[1] + 1):
                maximum(a)
            for u in range(STEPS):
                for what, i in dve_at[u]:
                    job(what, i)
                if u < NB:
                    for a in a_at[u]:
                        maximum(a)

            dve.wait_ge(dve_step, steps[0])
            link(dve.tensor_copy(idx_f[:, :, :], top_i[:, :, 0:TOPK]))
            onehot_v = onehot[:, :, :, :].rearrange("p t k e -> p (t k) e")
            dve.wait_ge(summed, NB)
            link(dve.tensor_tensor(onehot_v, iota_e[:, :].unsqueeze(1).broadcast_to([P, TILES * TOPK, EXPERTS]),
                                   idx_f[:, :, :].rearrange("p t k -> p (t k)").unsqueeze(2).broadcast_to(
                                       [P, TILES * TOPK, EXPERTS]), ALU.is_equal))
            with nc.allow_low_precision(reason="a token chooses an expert once or not: 0 or 1"):
                dve.tensor_reduce(chosen[:, :, :], onehot[:, :, :, :].rearrange("p t k e -> p t e k"),
                                  X, ALU.add).then_inc(chosen_ready, 1)
            dve.wait_ge(ranked, 1)
            counts = ps[:, 6, 256:256 + EXPERTS]
            ranks = ps[:, 6, 0:TILES * EXPERTS].rearrange("p (t e) -> p t e", t=TILES)
            link(dve.tensor_scalar(count_i[:, 0, :], counts, float(P - 1), None, ALU.add))
            link(dve.tensor_scalar(count_i[:, 1, :], count_i[:, 0, :], 7, None, ALU.arith_shift_right))
            link(dve.tensor_copy(nblk[:, :], count_i[:, 1, :]))
            link(dve.tensor_tensor_scan(nblk_end[:, :], nblk[:, :], zeros[:, 0:EXPERTS], 0.0, ALU.add, ALU.add))
            link(dve.tensor_tensor(nblk_start[:, :], nblk_end[:, :], nblk[:, :], ALU.subtract))
            link(dve.scalar_tensor_tensor(out=slot_te[:, :, :],
                                          in0=nblk_start[:, :].unsqueeze(1).broadcast_to([P, TILES, EXPERTS]),
                                          scalar=float(P), in1=ranks, op0=ALU.mult, op1=ALU.add))
            link(dve.tensor_tensor(slot_of[:, :, :, :], onehot[:, :, :, :],
                                   slot_te[:, :, :].unsqueeze(2).broadcast_to([P, TILES, TOPK, EXPERTS]), ALU.mult))
            link(dve.tensor_reduce(slot_f[:, :], slot_of[:, :, :, :].rearrange("p t k e -> p (t k) e"), X, ALU.add))
            dve.tensor_copy(slot_i[:, :], slot_f[:, :]).then_inc(slots_ready, 1)

            def shared(n):
                chunk, inner = n // 2, n % 2
                cols = slice(chunk * 512, (chunk + 1) * 512)
                dve.wait_ge(shared_silu, n + 1)
                dve.tensor_tensor(shared_act[:, inner, cols], shared_sig[:, inner, cols], ps[:, 2 * (n % 3) + 1, :],
                                  ALU.mult).then_inc(shared_ready, 1)

            shared(0)
            dve.wait_ge(base_ready, TILES)
            link(dve.tensor_tensor(below[:, :, :], nblk_end[0:1, :].unsqueeze(1).broadcast_to([1, MAX_BLOCKS, EXPERTS]),
                                   iota_b[:, :].unsqueeze(2).broadcast_to([1, MAX_BLOCKS, EXPERTS]), ALU.is_le))
            link(dve.tensor_reduce(expert_f[:, :], below[:, :, :], X, ALU.add))
            note(dve.tensor_scalar(w1_off[:, :], expert_f[:, :], float(EXPERTS - 1), float(DC * D), ALU.min, ALU.mult))
            dve.tensor_scalar(w2_off[:, :], expert_f[:, :], float(EXPERTS - 1), float(D), ALU.min,
                              ALU.mult).then_inc(offsets_ready, 1)
            for n in range(1, 4):
                shared(n)
            dve.wait_ge(top_exped, 1)
            link(dve.tensor_reduce(top_sum[:, :], top_e[:, :, :], X, ALU.add))
            link(dve.reciprocal(top_sum[:, :], top_sum[:, :]))
            note(dve.tensor_tensor(top_w[:, :, :], top_e[:, :, :],
                                   top_sum[:, :].unsqueeze(2).broadcast_to([P, TILES, TOPK]), ALU.mult))
            for t in range(TILES):
                dve.wait_ge(shared_down, t + 1)
                dve.wait_ge(base_ready, t + 1)
                dve.tensor_tensor(base[:, t, :], base[:, t, :], ps[:, 6 + t % 2, 0:D],
                                  ALU.add).then_inc(shared_added, 1)

            def turn_x_copy(b, n, r):
                dve.wait_ge(xs_turned, b + 1)
                dve.tensor_copy(xs_feat[:, r, :, :].rearrange("p c q -> p (c q)"), ps[:, 2 + n % 2, 0:D]).then_inc(xs_ready, 1)

            def step(b, n, r, q):
                if 1 <= n <= MAX_BLOCKS:
                    dve.wait_ge(act_turned, b)
                    dve.tensor_copy(act_feat[:, (r - 1) % RING, :], ps[:, 4 + (n - 1) % 2, 0:P]).then_inc(act_feat_ready, 1)
                if n + 1 < MAX_BLOCKS:
                    turn_x_copy(b + 1, n + 1, (r + 1) % RING)
                if n < MAX_BLOCKS:
                    dve.wait_ge(silu_ready, b + 1)
                    dve.tensor_tensor(act_sb[:, r, :], silu_sb[:, r, :], ps[:, n % 2, P:2 * P], ALU.mult).then_inc(act_ready, 1)

            turn_x_copy(0, 0, 0)
            over_blocks(dve, step)

            for t in range(TILES):
                dve.wait_ge(row_gathered[t], 16 * TOPK)
                for k in range(TOPK):
                    ins = dve.scalar_tensor_tensor(out=base[:, t, :], in0=gathered[:, TOPK * t + k, :],
                                                   scalar=top_w[:, t, k:k + 1], in1=base[:, t, :],
                                                   op0=ALU.mult, op1=ALU.add)
                    if k < TOPK - 1:
                        link(ins)
                    else:
                        ins.then_inc(combined, 1)


_INS = ["L0_attn_x", "L0_attn_w_attn", "L0_attn_w_proj", "L0_ffn_norm_w", "L0_ffn_router_w", "L0_ffn_w1",
        "L0_ffn_w2", "L0_ffn_sg", "L0_ffn_su", "L0_ffn_sd"]


def kernel(**inputs):
    import numpy as _np
    import concourse.bacc as _bacc
    from concourse import mybir as _mybir
    from concourse.bass_utils import run_bass_kernel_spmd as _run

    nc = _bacc.Bacc("TRN2", target_bir_lowering=False, num_devices=1)
    arrays, args = {}, []
    for name in _INS:
        a = _np.ascontiguousarray(inputs[name])
        arrays[f"in_{name}"] = a
        args.append(nc.dram_tensor(f"in_{name}", a.shape, _mybir.dt.from_np(a.dtype), kind="ExternalInput").ap())
    args.append(nc.dram_tensor("out_x", (1, T, D), F32, kind="ExternalOutput").ap())
    layer(nc, *args)
    r = _run(nc, [arrays], core_ids=[0])
    return r.results[0]["out_x"]
```

```python
from contextlib import ExitStack

import concourse.bass as bass
from concourse import mybir

F32 = mybir.dt.float32
F32R = mybir.dt.float32r
BF16 = mybir.dt.bfloat16
I32 = mybir.dt.int32
U32 = mybir.dt.uint32
ALU = mybir.AluOpType
ACT = mybir.ActivationFunctionType
X = mybir.AxisListType.X

P = 128
T, D = 1024, 256
TILES = T // P
DC = D // P
HEADS, HD = 16, 16
QK_SCALE = HD ** -0.5
PARTS = 6
ROWS = 2 + PARTS * HD
VW = HD + 1
EXPERTS, TOPK, INNER = 32, 4, 128
MAX_BLOCKS = (T * TOPK + EXPERTS * (P - 1)) // P
SLOTS = MAX_BLOCKS * P
RING = 4
OFF_PAD = 5
P_RING = 4
EPS_LN, EPS_RMS = 1e-5, 1e-6
NEG = -1e30


def max_units():
    units, first, last = [], [], []
    for i in range(TILES):
        first.append(len(units))
        width = (i + 1) * P
        w0 = min(width, 512)
        per = 512 // w0
        for a in range(0, HEADS, per):
            units.append((i, list(range(a, a + per)), 0, w0, 0, width <= 512))
        if width > 512:
            w1 = width - 512
            per = 512 // w1
            for a in range(0, HEADS, per):
                units.append((i, list(range(a, a + per)), 512, w1, 1, True))
        last.append(len(units) - 1)
    return units, first, last


def prob_units():
    units, first = [], []
    for i in range(TILES):
        first.append(len(units))
        per = 2 if i < 4 else 1
        for h in range(0, HEADS, per):
            units.append((i, list(range(h, h + per))))
    return units, first


def layer(nc, x, w_attn, w_proj, norm_w, router_w, w1, w2, sg, su, sd, out):
    A_UNITS, A_FIRST, A_LAST = max_units()
    B_UNITS, B_FIRST = prob_units()
    NB = len(B_UNITS)
    STEPS = NB + 8

    a_at = [[] for _ in range(STEPS)]
    pe_at = [[] for _ in range(STEPS)]
    dve_at = [[] for _ in range(STEPS)]
    act_at = [[] for _ in range(STEPS)]
    act_first = [[] for _ in range(STEPS)]
    pool_at = [[] for _ in range(STEPS)]
    for i in range(TILES - 2):
        n = B_FIRST[i + 1] - B_FIRST[i]
        todo = list(range(A_FIRST[i + 2], A_LAST[i + 2] + 1))
        for a, unit in enumerate(todo):
            a_at[B_FIRST[i] + a * n // len(todo)].append(unit)
    for i in range(TILES):
        s = (B_FIRST[i + 1] if i + 1 < TILES else NB) + 1
        act_first[s].append(i)
        pe_at[s].append(("o_turn", i))
        dve_at[s + 1].append(("norm", i))
        pe_at[s + 1].append(("y_turn", i))
        act_at[s + 2].append(("y_copy", i))
        pe_at[s + 2].append(("proj", i))
        dve_at[s + 3].append(("residual", i))
        pool_at[s + 3].append(("rstd", i))
        dve_at[s + 4].append(("h", i))
        pe_at[s + 4].append(("h_turn", i))
        act_at[s + 5].append(("h_copy", i))
        pe_at[s + 5].append(("logits", i))
        dve_at[s + 6].append(("top", i))
        if i:
            s = B_FIRST[i - 1]
            if i >= 4:
                dve_at[s + 1].append(("max_join", i))
            pe_at[s + 3].append(("max_turn", i))
            dve_at[s + 4].append(("max_copy", i))

    order = [("max_turn", 0)] + [job for jobs in pe_at for job in jobs]
    turn = {job: n for n, job in enumerate(order)}

    ctx = ExitStack()
    with ctx:
        start = nc.sbuf_base + (-nc.sbuf_base) % 64
        end = nc.sbuf_usable_end
        cursor = [start]

        def sb(name, shape, dt, at=None):
            size = int(mybir.dt.size(dt))
            for n in shape[1:]:
                size *= n
            if at is None:
                at = cursor[0]
                cursor[0] += size + (-size) % 64
                assert cursor[0] <= end, (name, cursor[0], end)
            return nc.alloc_sbuf_tensor_at(name, shape, dt, offset=at)

        KB = 1024
        w1_at = cursor[0]
        w1_sb = sb("w1_sb", [P, EXPERTS * DC * D], F32)
        gathered = sb("gathered", [P, TILES * TOPK, D], F32, w1_at)
        q_at = cursor[0]
        q_stack = sb("q_stack", [P, HEADS, T], BF16)
        w2_sb = sb("w2_sb", [P, EXPERTS * D], F32, q_at)
        k_at = cursor[0]
        k_stack = sb("k_stack", [P, HEADS, T], BF16)
        shared_sig = sb("shared_sig", [P, 2, T], F32, k_at)
        shared_act = sb("shared_act", [P, 2, T], F32, k_at + 8 * KB)
        ys_sb = sb("ys_sb", [P, RING, D], F32, k_at)
        silu_sb = sb("silu_sb", [P, RING, P], F32, k_at + 4 * KB)
        xs_tok = sb("xs_tok", [P, RING, D], F32, k_at + 16 * KB)
        xs_feat = sb("xs_feat", [P, RING, DC, P], F32, k_at + 20 * KB)
        act_sb = sb("act_sb", [P, RING, P], F32, k_at + 24 * KB)
        act_feat = sb("act_feat", [P, RING, P], F32, k_at + 26 * KB)
        v_ext = sb("v_ext", [P, TILES, HEADS, VW], F32)
        x_sb = sb("x_sb", [P, TILES, D], F32)
        tok_at = cursor[0]
        xn = sb("xn", [P, TILES, D], F32)
        h_tok = sb("h_tok", [P, TILES, D], F32, tok_at)
        base = x_sb
        feat_at = cursor[0]
        xn_feat = sb("xn_feat", [P, DC, T], F32)
        h_feat = sb("h_feat", [P, DC, T], F32, feat_at)
        st_at = cursor[0]
        qk_tok = sb("qk_tok", [P, 2, 2 * HEADS, ROWS], BF16)
        rest = sb("rest", [P, 2, 2 * HEADS, HD], F32)
        probs = sb("probs", [P, P_RING, T], F32, st_at)
        onehot = sb("onehot", [P, TILES, TOPK, EXPERTS], F32, st_at)
        slot_of = sb("slot_of", [P, TILES, TOPK, EXPERTS], F32, st_at + 4 * KB)
        below = sb("below", [1, MAX_BLOCKS, EXPERTS], F32, st_at + 8 * KB)
        pos_onehot = sb("pos_onehot", [P, TILES * TOPK, P], BF16, st_at)
        block_onehot = sb("block_onehot", [P, TILES * TOPK, MAX_BLOCKS], BF16, st_at + 8 * KB)
        block_row = sb("block_row", [P, 2, TILES * TOPK, MAX_BLOCKS], BF16, feat_at)
        wa_at = cursor[0]
        wa_sb = sb("wa_sb", [P, DC, 3 * D], F32)
        wp_sb = sb("wp_sb", [P, DC, D], F32)
        sg_sb = sb("sg_sb", [P, DC, D], F32)
        su_sb = sb("su_sb", [P, DC, D], F32)
        sd_sb = sb("sd_sb", [P, DC, D], F32)
        nw_sb = sb("nw_sb", [P, D], F32)
        zeros = sb("zeros", [P, D], F32)
        ident = sb("ident", [P, P], F32)
        ident_b = sb("ident_b", [P, P], BF16)
        before_b = sb("before_b", [P, P], BF16)
        ones_b = sb("ones_b", [P, P], BF16)
        future_b = sb("future_b", [P, P], BF16)
        router_sb = sb("router_sb", [EXPERTS, D], F32)
        router_feat = sb("router_feat", [P, DC, EXPERTS], F32)
        powers = sb("powers", [P, 16], F32)
        iota_row = sb("iota_row", [P, P], F32)
        iota_e, iota_b = iota_row[:, 0:EXPERTS], iota_row[0:1, 0:MAX_BLOCKS]
        partition = sb("partition", [P, 1], F32)
        spare_row = sb("spare_row", [P, MAX_BLOCKS], F32)
        row_base = sb("row_base", [P, TILES * TOPK], F32)
        stats = sb("stats", [P, TILES, 6], F32)
        mean_var = sb("mean_var", [P, TILES, 2], F32)
        var_eps = sb("var_eps", [P, TILES], F32)
        rstd = sb("rstd", [P, TILES], F32)
        row_max = sb("row_max", [P, 2, TILES, HEADS], F32)
        neg_max = sb("neg_max", [HEADS, 2, 2, P], BF16)
        denom = sb("denom", [P, HEADS], F32)
        o_sb = sb("o_sb", [P, 4, P], F32)
        y_tok = sb("y_tok", [P, D], F32)
        y_feat = sb("y_feat", [P, DC, P], F32)
        stats2 = sb("stats2", [P, 6], F32)
        mean_var2 = sb("mean_var2", [P, 2, 2], F32)
        var_args = sb("var_args", [P, 2, 2], F32)
        rstd2 = sb("rstd2", [P, 2, 2], F32)
        h_raw = sb("h_raw", [P, D], F32)
        ln2 = sb("ln2", [P, D], F32)
        logit_sb = sb("logit_sb", [P, TILES, EXPERTS], F32, wa_at)
        top_v = sb("top_v", [P, TILES, 8], F32, wa_at + 2 * KB)
        top_i = sb("top_i", [P, TILES, 8], U32, wa_at + 3 * KB)
        top_d = sb("top_d", [P, TILES, TOPK], F32)
        top_e = sb("top_e", [P, TILES, TOPK], F32)
        top_sum = sb("top_sum", [P, TILES], F32)
        top_w = sb("top_w", [P, TILES, TOPK], F32)
        idx_f = sb("idx_f", [P, TILES, TOPK], F32, wa_at + 5 * KB)
        chosen = sb("chosen", [P, TILES, EXPERTS], BF16, wa_at + 4 * KB)
        count_i = sb("count_i", [P, 2, EXPERTS], I32, wa_at + 5 * KB + 128)
        nblk = sb("nblk", [P, EXPERTS], F32)
        nblk_end = sb("nblk_end", [P, EXPERTS], F32)
        nblk_start = sb("nblk_start", [P, EXPERTS], F32)
        slot_te = sb("slot_te", [P, TILES, EXPERTS], F32, wa_at + KB)
        slot_f = sb("slot_f", [P, TILES * TOPK], F32, wa_at + 5 * KB + 384)
        slot_i = sb("slot_i", [P, TILES * TOPK], I32)
        expert_f = sb("expert_f", [1, MAX_BLOCKS], F32, wa_at + 5 * KB + 512)
        w_off = sb("w_off", [1, OFF_PAD + MAX_BLOCKS + RING], I32)
        place = sb("place", [P, 2, TILES * TOPK], I32)
        place_f = sb("place_f", [P, 2, TILES * TOPK], F32)
        unused = sb("unused", [P, MAX_BLOCKS], F32)
        row_i = sb("row_i", [P, MAX_BLOCKS], I32)

        xs_dram = nc.dram_tensor("xs_dram", [SLOTS, D], F32).ap()
        pair_dram = nc.dram_tensor("pair_dram", [T * TOPK + SLOTS, D], F32).ap()

        ps = ctx.enter_context(nc.psum_tensor("ps", [P, 8, 512], F32))

        def sem(name):
            return ctx.enter_context(nc.semaphore(name))

        x_loaded = [sem(f"x_loaded{n}") for n in range(4)]
        wa_loaded, wp_loaded, router_loaded = sem("wa_loaded"), sem("wp_loaded"), sem("router_loaded")
        nw_loaded, shared_loaded = sem("nw_loaded"), sem("shared_loaded")
        w1_loaded, w2_loaded, xs_cleared = sem("w1_loaded"), sem("w2_loaded"), sem("xs_cleared")
        zeros_ready, consts, stack_consts = sem("zeros_ready"), sem("consts"), sem("stack_consts")
        pool_step, dve_step = sem("pool_step"), sem("dve_step")
        stats_ready, rstd_ready, xn_ready = sem("stats_ready"), sem("rstd_ready"), sem("xn_ready")
        router_turned, router_ready = sem("router_turned"), sem("router_ready")
        xn_turned, xn_feat_ready = sem("xn_turned"), sem("xn_feat_ready")
        qk_made, v_made = sem("qk_made"), sem("v_made")
        a_ready, rest_ready = sem("a_ready"), sem("rest_ready")
        b_ready, c_ready, copies_ready, v_ready = sem("b_ready"), sem("c_ready"), sem("copies_ready"), sem("v_ready")
        stacked = [sem("stacked0"), sem("stacked1")]
        stack_ready = [sem("stack_ready_act"), sem("stack_ready_dve")]
        rows_scored, row_maxed, max_joined = sem("rows_scored"), sem("row_maxed"), sem("max_joined")
        max_placed = [sem("max_placed0"), sem("max_placed1")]
        scored, exped, masked, summed = sem("scored"), sem("exped"), sem("masked"), sem("summed")
        sums_cleared, o_copied = sem("sums_cleared"), sem("o_copied")
        misc_made, misc_used = sem("misc_made"), sem("misc_used")
        var_ready, rstd2_ready, h_ready = sem("var_ready"), sem("rstd2_ready"), sem("h_ready")
        base_ready, top_ready, top_exped = sem("base_ready"), sem("top_ready"), sem("top_exped")
        chosen_ready, ranked, slots_ready = sem("chosen_ready"), sem("ranked"), sem("slots_ready")
        offsets_ready, places_ready, places_scaled = sem("offsets_ready"), sem("places_ready"), sem("places_scaled")
        rows_found, rows_ready = sem("rows_found"), sem("rows_ready")
        shared_up, shared_silu, shared_ready = sem("shared_up"), sem("shared_silu"), sem("shared_ready")
        shared_down, shared_added = sem("shared_down"), sem("shared_added")
        scattered = sem("scattered")
        xs_loaded = [sem(f"xs_loaded{r}") for r in range(RING)]
        ys_stored = [sem(f"ys_stored{r}") for r in range(RING)]
        xs_turned, xs_ready, gate_up = sem("xs_turned"), sem("xs_ready"), sem("gate_up")
        silu_ready, act_ready, act_turned = sem("silu_ready"), sem("act_ready"), sem("act_turned")
        act_feat_ready, down, ys_ready = sem("act_feat_ready"), sem("down"), sem("ys_ready")
        row_gathered = [sem(f"row_gathered{t}") for t in range(TILES)]
        combined, stored = sem("combined"), sem("stored")

        x_d = x.rearrange("a (t p) d -> p (a t) d", p=P)
        out_d = out.rearrange("a (t p) d -> p (a t) d", p=P)

        def part(j, heads, n, count=1, step=1):
            v = qk_tok[:, j % 2, heads, 2:ROWS].rearrange("p h (s d) -> p h s d", s=PARTS)
            return v[:, :, n:n + (count - 1) * step + 1:step, :]

        queries, keys = slice(0, HEADS), slice(HEADS, 2 * HEADS)

        def over_blocks(engine, step):
            head = 2 * RING - 1
            turns = (MAX_BLOCKS - RING - head) // RING
            for b in range(head):
                step(b, b, b % RING, b // RING)
            with engine.Fori(0, turns) as it:
                for n in range(head, head + RING):
                    step(it * RING + n, n, n % RING, it + n // RING)
            for b in range(head + turns * RING, MAX_BLOCKS + 2):
                step(b, b, b % RING, b // RING)

        block = ctx.enter_context(nc.Block())

        @block.sync
        def _(sp):
            for n in range(4):
                sp.dma_start(x_sb[:, 2 * n:2 * n + 2, :], x_d[:, 2 * n:2 * n + 2, :]).then_inc(x_loaded[n], 16)
            sp.dma_start(router_sb[:, :], router_w).then_inc(router_loaded, 16)
            sp.dma_start(wa_sb[:, :, :], w_attn.rearrange("(c p) n -> p c n", p=P)).then_inc(wa_loaded, 16)
            sp.dma_start(wp_sb[:, :, :], w_proj.rearrange("(c p) n -> p c n", p=P)).then_inc(wp_loaded, 16)
            sp.dma_start(nw_sb[:, :], norm_w.rearrange("(a n) -> a n", a=1).broadcast_to([P, D])).then_inc(nw_loaded, 16)
            for dst, src in ((sg_sb, sg), (su_sb, su), (sd_sb, sd)):
                sp.dma_start(dst[:, :, :], src.rearrange("(c p) n -> p c n", p=P)).then_inc(shared_loaded, 16)
            sp.wait_ge(zeros_ready, 1)
            sp.dma_start(xs_dram.rearrange("(b p) d -> p b d", p=P),
                         zeros[:, :].unsqueeze(1).broadcast_to([P, MAX_BLOCKS, D])).then_inc(xs_cleared, 16)
            w1_v = w1_sb[:, :].rearrange("p (c e n) -> p c e n", e=EXPERTS, c=DC)
            for c in range(DC):
                sp.dma_start(w1_v[:, c, :, :], w1[:, c * P:(c + 1) * P, :].rearrange("e p n -> p e n")).then_inc(w1_loaded, 16)
            for i in range(TILES):
                sp.wait_ge(misc_used, turn["max_turn", i] + 1)
                sp.wait_ge(rows_scored, A_LAST[i] + 1)
                for part in range(2):
                    sp.dma_start(q_stack[part:part + 1, :, i * P:(i + 1) * P],
                                 neg_max[:, i % 2, part, :]).then_inc(max_placed[i % 2], 16)
            sp.wait_ge(summed, NB)
            sp.dma_start(w2_sb[:, :].rearrange("p (e n) -> p e n", e=EXPERTS),
                         w2.rearrange("e p n -> p e n")).then_inc(w2_loaded, 16)

            def load(b, r):
                sp.dma_start(xs_tok[:, r, :], xs_dram[bass.ts(b, P), :]).then_inc(xs_loaded[r], 16)

            sp.wait_ge(scattered, 16 * TILES * TOPK)
            for b in range(RING):
                load(b, b)

            def step(b, n, r, q):
                if n + RING < MAX_BLOCKS:
                    sp.wait_ge(xs_turned, b + 1)
                    load(b + RING, r)

            over_blocks(sp, step)
            for r in range(RING):
                sp.wait_ge(ys_stored[r], 16 * len(range(r, MAX_BLOCKS, RING)))
            for t in range(TILES):
                sp.dma_start(gathered[:, TOPK * t:TOPK * (t + 1), :],
                             pair_dram[TOPK * t * P:TOPK * (t + 1) * P, :].rearrange("(k p) d -> p k d", p=P)
                             ).then_inc(row_gathered[t], 16)
            for t in range(TILES):
                sp.wait_ge(combined, t + 1)
                sp.dma_start(out_d[:, t, :], base[:, t, :]).then_inc(stored, 16)
            sp.wait_ge(stored, 16 * TILES)

        @block.gpsimd
        def _(pool):
            steps = [0]

            def link(ins):
                steps[0] += 1
                ins.then_inc(pool_step, 1)
                pool.wait_ge(pool_step, steps[0])

            pool.memset(zeros[:, :], 0.0).then_inc(zeros_ready, 1)
            pool.memset(powers[:, :], -0.5)
            pool.memset(ones_b[:, :], 1.0)
            link(pool.memset(ident[:, :], 0.0))
            link(pool.affine_select(out=ident[:, :], in_=ident[:, :], compare_op=ALU.not_equal, fill=1.0, base=0,
                                    pattern=[[-1, P]], channel_multiplier=1))
            pool.tensor_copy(ident_b[:, :], ident[:, :])
            link(pool.memset(future_b[:, :], 0.0))
            pool.affine_select(out=future_b[:, :], in_=future_b[:, :], compare_op=ALU.is_ge, fill=NEG, base=0,
                               pattern=[[-1, P]], channel_multiplier=1)
            pool.affine_select(out=before_b[:, :], in_=ones_b[:, :], compare_op=ALU.is_gt, fill=0.0, base=0,
                               pattern=[[1, P]], channel_multiplier=-1)
            pool.iota(iota_row[:, :], [[1, P]], base=0, channel_multiplier=0, allow_small_or_imprecise_dtypes=True)
            pool.iota(partition[:, :], [[0, 1]], base=0, channel_multiplier=1, allow_small_or_imprecise_dtypes=True)
            pool.iota(spare_row[:, :], [[P, MAX_BLOCKS]], base=T * TOPK + P, channel_multiplier=1,
                      allow_small_or_imprecise_dtypes=True)
            link(pool.iota(row_base[:, :], [[P, TILES * TOPK]], base=P, channel_multiplier=0,
                           allow_small_or_imprecise_dtypes=True))
            pool.memset(v_ext[:, :, :, HD:VW], 1.0).then_inc(consts, 1)
            for g in range(2):
                pool.wait_ge(stats_ready, g + 1)
                pool.tensor_tensor(rstd[:, 4 * g:4 * g + 4], var_eps[:, 4 * g:4 * g + 4], powers[:, 0:4],
                                   ALU.pow).then_inc(rstd_ready, 1)

            both = slice(0, 2 * HEADS)
            for j in range(TILES):
                pool.wait_ge(rest_ready, 2 * (j + 1))
                pool.tensor_copy(part(j, both, 4), rest[:, j % 2, :, :].unsqueeze(2)).then_inc(b_ready, 1)
                pool.wait_ge(b_ready, j + 1)
                pool.tensor_copy(part(j, queries, 3), part(j, queries, 4))
                pool.tensor_copy(part(j, keys, 2), part(j, keys, 4)).then_inc(copies_ready, 1)

            def mask(u):
                i, heads = B_UNITS[u]
                pool.wait_ge(exped, u + 1)
                v = probs[:, u % P_RING, :].rearrange("p (a q) -> p a q", a=2 if len(heads) == 2 else 1)
                v = v[:, :, i * P:(i + 1) * P]
                pool.affine_select(out=v, in_=v, compare_op=ALU.is_ge, fill=0.0, base=0,
                                   pattern=[[0, len(heads)], [1, P]], channel_multiplier=-1).then_inc(masked, 1)

            for u in range(STEPS):
                if u < NB:
                    mask(u)
                for _, i in pool_at[u]:
                    pool.wait_ge(var_ready, i + 1)
                    pool.tensor_tensor(rstd2[:, i % 2, :], var_args[:, i % 2, :], powers[:, 0:2],
                                       ALU.pow).then_inc(rstd2_ready, 1)
                    pool.wait_ge(rstd2_ready, i + 1)
                    link(pool.tensor_scalar(ln2[:, :], x_sb[:, i, :], mean_var2[:, i % 2, 0:1], rstd2[:, i % 2, 0:1],
                                            ALU.subtract, ALU.mult))
                    pool.wait_ge(h_ready, i + 1)
                    pool.tensor_tensor(base[:, i, :], x_sb[:, i, :], ln2[:, :], ALU.add).then_inc(base_ready, 1)
                    if i + 1 < TILES:
                        pool.wait_ge(base_ready, i + 1)

            pool.wait_ge(slots_ready, 1)
            pool.wait_ge(xs_cleared, 16)
            for n in range(TILES * TOPK):
                pool.indirect_dma_start(xs_dram, bass.IndirectOffsetOnAxis(slot_i[:, n:n + 1], 0),
                                        h_tok[:, n // TOPK, :], None).then_inc(scattered, 16)

            pool.wait_ge(rows_ready, 1)
            for b in range(MAX_BLOCKS):
                pool.wait_ge(ys_ready, b + 1)
                pool.indirect_dma_start(pair_dram, bass.IndirectOffsetOnAxis(row_i[:, b:b + 1], 0),
                                        ys_sb[:, b % RING, :], None).then_inc(ys_stored[b % RING], 16)

        @block.tensor
        def _(pe):
            pe.wait_ge(consts, 1)
            pe.wait_ge(router_loaded, 16)
            for c in range(DC):
                last = pe.transpose(ps[:, 7, c * EXPERTS:(c + 1) * EXPERTS], router_sb[:, c * P:(c + 1) * P],
                                    ident[0:EXPERTS, 0:EXPERTS])
            last.then_inc(router_turned, 1)

            def turn_xn(j):
                pe.wait_ge(xn_ready, j + 1)
                if j >= 2:
                    pe.wait_ge(xn_feat_ready, j - 1)
                for c in range(DC):
                    last = pe.transpose(ps[:, j % 2, c * P:(c + 1) * P], xn[:, j, c * P:(c + 1) * P], ident[:, :])
                last.then_inc(xn_turned, 1)

            def project(j):
                pe.wait_ge(xn_feat_ready, j + 1)
                if j >= 2:
                    pe.wait_ge(rest_ready, 2 * (j - 1))
                    pe.wait_ge(v_ready, j - 1)
                for c in range(DC):
                    last = pe.matmul(ps[:, 2 + j % 2, :], xn_feat[:, c, j * P:(j + 1) * P], wa_sb[:, c, 0:2 * D],
                                     start=(c == 0), stop=(c == DC - 1))
                last.then_inc(qk_made, 1)
                for c in range(DC):
                    last = pe.matmul(ps[:, 4 + j % 2, 0:D], xn_feat[:, c, j * P:(j + 1) * P], wa_sb[:, c, 2 * D:3 * D],
                                     start=(c == 0), stop=(c == DC - 1))
                last.then_inc(v_made, 1)

            def stack(j):
                pe.wait_ge(copies_ready, j + 1)
                pe.wait_ge(c_ready, 2 * (j + 1))
                for g in range(4):
                    n = 2 * j + g // 2
                    if n:
                        pe.wait_ge(stack_ready[g % 2], n)
                    bank = ps[0:ROWS, 6 + g % 2, :].bitcast(BF16)
                    for h in range(8):
                        last = pe.transpose(bank[:, h * P:(h + 1) * P], qk_tok[:, j % 2, 8 * g + h, :], ident_b[:, :])
                    last.then_inc(stacked[g % 2], 1)

            turn_xn(0)
            pe.wait_ge(wa_loaded, 16)
            pe.wait_ge(router_ready, 1)
            for j in range(TILES):
                if j + 1 < TILES:
                    turn_xn(j + 1)
                project(j)
                if j:
                    stack(j - 1)
            stack(TILES - 1)

            pe.wait_ge(xn_feat_ready, TILES)
            pe.wait_ge(v_ready, TILES)
            for g in range(2):
                pe.wait_ge(stack_ready[g], 2 * TILES)

            def score_rows(a):
                i, heads, k0, kw, part, diagonal = A_UNITS[a]
                if a >= 2:
                    pe.wait_ge(row_maxed, a - 1)
                for n, h in enumerate(heads):
                    last = pe.matmul(ps[:, a % 2, n * kw:(n + 1) * kw], q_stack[0:ROWS, h, i * P:(i + 1) * P],
                                     k_stack[0:ROWS, h, k0:k0 + kw], start=True, stop=not diagonal)
                    if diagonal:
                        last = pe.matmul(ps[:, a % 2, (n + 1) * kw - P:(n + 1) * kw], ident_b[:, :], future_b[:, :],
                                         start=False, stop=True)
                last.then_inc(rows_scored, 1)

            def turn_max(i):
                if i >= 4:
                    pe.wait_ge(max_joined, i - 3)
                else:
                    pe.wait_ge(row_maxed, A_LAST[i] + 1)
                return pe.transpose(ps[0:HEADS, 7, 0:P], row_max[:, 0, i, :], ident[:, :])

            def score_keys(u):
                i, heads = B_UNITS[u]
                if u >= 2:
                    pe.wait_ge(exped, u - 1)
                if u == B_FIRST[i]:
                    pe.wait_ge(max_placed[i % 2], 32 * (i // 2 + 1))
                bank = 2 + 2 * (u % 2)
                for jt in range(i + 1):
                    for n, h in enumerate(heads):
                        at = 512 * n + jt * P
                        last = pe.matmul(ps[:, bank + at // 512, at % 512:at % 512 + P],
                                         k_stack[0:ROWS, h, jt * P:(jt + 1) * P],
                                         q_stack[0:ROWS, h, i * P:(i + 1) * P], start=True, stop=True)
                last.then_inc(scored, 1)

            def sum_values(u):
                i, heads = B_UNITS[u]
                if len(heads) == 1:
                    if u % 2 == 0:
                        return
                    heads = [heads[0] - 1, heads[0]]
                pe.wait_ge(masked, u + 1)
                if heads[0] == 0 and i:
                    pe.wait_ge(o_copied, i)
                for jt in range(i + 1):
                    for n, h in enumerate(heads):
                        if i < 4:
                            p = probs[:, u % P_RING, 512 * n + jt * P:512 * n + (jt + 1) * P]
                        else:
                            p = probs[:, (u - 1 + n) % P_RING, jt * P:(jt + 1) * P]
                        c = 32 * (h % 4)
                        last = pe.matmul(ps[c:c + VW, 6, (h // 4) * P:(h // 4 + 1) * P], v_ext[:, jt, h, :], p,
                                         start=(jt == 0), stop=(jt == i))
                last.then_inc(summed, 1 if i < 4 else 2)

            def job(what, i):
                if turn[what, i]:
                    pe.wait_ge(misc_used, turn[what, i])
                if what == "max_turn":
                    last = turn_max(i)
                elif what == "o_turn":
                    pe.wait_ge(o_copied, i + 1)
                    for g in range(4):
                        last = pe.transpose(ps[:, 7, g * P:(g + 1) * P], o_sb[:, g, :], ident[:, :])
                elif what == "y_turn":
                    for c in range(DC):
                        last = pe.transpose(ps[:, 7, c * P:(c + 1) * P], y_tok[:, c * P:(c + 1) * P], ident[:, :])
                elif what == "proj":
                    pe.wait_ge(wp_loaded, 16)
                    for c in range(DC):
                        last = pe.matmul(ps[:, 7, D:2 * D], y_feat[:, c, :], wp_sb[:, c, :],
                                         start=(c == 0), stop=(c == DC - 1))
                elif what == "h_turn":
                    pe.wait_ge(h_ready, i + 1)
                    for c in range(DC):
                        last = pe.transpose(ps[:, 7, c * P:(c + 1) * P], h_tok[:, i, c * P:(c + 1) * P], ident[:, :])
                elif what == "logits":
                    for c in range(DC):
                        last = pe.matmul(ps[:, 7, D:D + EXPERTS], h_feat[:, c, i * P:(i + 1) * P], router_feat[:, c, :],
                                         start=(c == 0), stop=(c == DC - 1))
                last.then_inc(misc_made, 1)

            for a in range(A_LAST[0] + 1):
                score_rows(a)
            job("max_turn", 0)
            pe.wait_ge(sums_cleared, 1)
            for a in range(A_FIRST[1], A_LAST[1] + 1):
                score_rows(a)
            score_keys(0)
            for u in range(STEPS):
                if u + 1 < NB:
                    score_keys(u + 1)
                for a in a_at[u]:
                    score_rows(a)
                if 1 <= u <= NB:
                    sum_values(u - 1)
                for what, i in pe_at[u]:
                    job(what, i)

            pe.wait_ge(shared_loaded, 48)
            pe.wait_ge(row_maxed, len(A_UNITS))
            pe.wait_ge(exped, NB)
            pe.wait_ge(misc_used, len(order))

            def up(n):
                chunk, inner = n // 2, n % 2
                bank = 2 * (n % 3)
                if n >= 3:
                    pe.wait_ge(shared_ready, n - 2)
                for w, b in ((sg_sb, bank), (su_sb, bank + 1)):
                    for c in range(DC):
                        last = pe.matmul(ps[:, b, :], w[:, c, inner * P:(inner + 1) * P],
                                         h_feat[:, c, chunk * 512:(chunk + 1) * 512], start=(c == 0), stop=(c == DC - 1))
                last.then_inc(shared_up, 1)

            up(0)
            pe.wait_ge(chosen_ready, 1)
            ranks = ps[:, 6, 0:TILES * EXPERTS].rearrange("p (t e) -> p t e", t=TILES)
            pe.matmul(ranks, before_b[:, :], chosen[:, :, :], start=True, stop=False)
            for t in range(TILES - 1):
                n = TILES - 1 - t
                pe.matmul(ranks[:, t + 1:, :], ones_b[:, :], chosen[:, t:t + 1, :].broadcast_to([P, n, EXPERTS]),
                          start=False, stop=(t == TILES - 2))
            for t in range(TILES):
                last = pe.matmul(ps[:, 6, 256:256 + EXPERTS], ones_b[:, :], chosen[:, t, :],
                                 start=(t == 0), stop=(t == TILES - 1))
            last.then_inc(ranked, 1)
            for n in range(1, 4):
                up(n)
            pe.wait_ge(slots_ready, 1)
            for t in range(TILES):
                if t % 4 == 0:
                    pe.wait_ge(shared_ready, 2 * (t // 4) + 2)
                if t >= 2:
                    pe.wait_ge(shared_added, t - 1)
                for c in range(2):
                    last = pe.matmul(ps[:, 6 + t % 2, 0:D], shared_act[:, c, t * P:(t + 1) * P],
                                     sd_sb[:, c, :], start=(c == 0), stop=(c == 1))
                last.then_inc(shared_down, 1)

            table = ps[:, 4, 0:MAX_BLOCKS]
            pe.wait_ge(shared_ready, 4)
            pe.wait_ge(places_ready, 3)
            pe.wait_ge(places_scaled, 1)
            for n in range(TILES * TOPK):
                for half in range(2):
                    last = pe.matmul(table, pos_onehot[:, n, :], block_row[:, half, n, :], start=(n + half == 0),
                                     stop=(n + half == TILES * TOPK))
            last.then_inc(rows_found, 1)

            pe.wait_ge(w1_loaded, 16 * DC)
            pe.wait_ge(w2_loaded, 16)
            pe.wait_ge(offsets_ready, 1)
            pe.wait_ge(shared_ready, 4)

            def turn_x(b, n, r, q):
                pe.wait_ge(xs_loaded[r], 16 * q + 16)
                for c in range(DC):
                    last = pe.transpose(ps[:, 2 + n % 2, c * P:(c + 1) * P], xs_tok[:, r, c * P:(c + 1) * P], ident[:, :])
                last.then_inc(xs_turned, 1)

            offsets = [pe.alloc_register(f"offset{n}") for n in range(2 * RING)]

            def group(b):
                pe.load(offsets, w_off[0:1, bass.ds(b - RING + OFF_PAD, 2 * RING)])

            def offset(back):
                return pe.snap(offsets[RING + back], min_val=0, max_val=(EXPERTS - 1) * D)

            def step(b, n, r, q):
                g = (r - (RING - 1)) % RING
                if g == 0:
                    group(b)
                if n < MAX_BLOCKS:
                    at = offset(g)
                    pe.wait_ge(xs_ready, b + 1)
                    for c in range(DC):
                        last = pe.matmul(ps[:, n % 2, 0:D], xs_feat[:, r, c, :], w1_sb[:, bass.ds(at + c * EXPERTS * D, D)],
                                         start=(c == 0), stop=(c == DC - 1))
                    last.then_inc(gate_up, 1)
                if 1 <= n <= MAX_BLOCKS:
                    pe.wait_ge(act_ready, b)
                    pe.transpose(ps[:, 4 + (n - 1) % 2, 0:P], act_sb[:, (r - 1) % RING, :], ident[:, :]).then_inc(act_turned, 1)
                if n + 1 < MAX_BLOCKS:
                    turn_x(b + 1, n + 1, (r + 1) % RING, q + int(r == RING - 1))
                if n >= 2:
                    at = offset(g - 2)
                    pe.wait_ge(act_feat_ready, b - 1)
                    pe.matmul(ps[:, 6 + n % 2, 0:D], act_feat[:, (r - 2) % RING, :], w2_sb[:, bass.ds(at, D)],
                              start=True, stop=True).then_inc(down, 1)

            turn_x(0, 0, 0, 0)
            group(-1)
            over_blocks(pe, step)

        @block.scalar
        def _(act):
            act.wait_ge(router_turned, 1)
            act.activation(router_feat[:, :, :].rearrange("p c e -> p (c e)"), ps[:, 7, 0:DC * EXPERTS],
                           ACT.Copy).then_inc(router_ready, 1)

            def turn_xn_copy(j):
                act.wait_ge(xn_turned, j + 1)
                act.activation(xn_feat[:, :, j * P:(j + 1) * P],
                               ps[:, j % 2, 0:D].rearrange("p (c q) -> p c q", c=DC), ACT.Copy).then_inc(xn_feat_ready, 1)

            turn_xn_copy(0)
            for j in range(TILES + 1):
                if j + 1 < TILES:
                    turn_xn_copy(j + 1)
                if j < TILES:
                    act.wait_ge(qk_made, j + 1)
                    if j == 0:
                        act.wait_ge(stack_consts, 1)
                    if j >= 2:
                        act.wait_ge(stacked[1], 2 * (j - 1))
                    for heads, first, step, scale in ((queries, 0, 1, QK_SCALE), (keys, 1, 2, 1.0)):
                        act.activation(part(j, heads, first, 3, step),
                                       ps[:, 2 + j % 2, heads.start * HD:heads.stop * HD].rearrange(
                                           "p (h d) -> p h d", d=HD).unsqueeze(2).broadcast_to([P, HEADS, 3, HD]),
                                       ACT.Copy, scale=scale).then_inc(a_ready, 1)
                if j:
                    for g, dst in enumerate((q_stack, k_stack)):
                        act.wait_ge(stacked[0], 2 * (j - 1) + g + 1)
                        act.activation(dst[0:ROWS, 0:8, (j - 1) * P:j * P],
                                       ps[0:ROWS, 6, :].bitcast(BF16).rearrange("p (h q) -> p h q", h=8),
                                       ACT.Copy).then_inc(stack_ready[0], 1)

            def exp(u):
                i, heads = B_UNITS[u]
                act.wait_ge(scored, u + 1)
                if u >= P_RING:
                    act.wait_ge(summed, u - P_RING + 1)
                bank = 2 + 2 * (u % 2)
                if len(heads) == 2:
                    n = (i + 1) * P
                    act.activation(probs[:, u % P_RING, :].rearrange("p (a q) -> p a q", a=2)[:, :, 0:n],
                                   ps[:, bank:bank + 2, 0:n], ACT.Exp).then_inc(exped, 1)
                else:
                    n = (i + 1) * P
                    act.activation(probs[:, u % P_RING, 0:n],
                                   ps[:, bank:bank + 2, :].rearrange("p a q -> p (a q)")[:, 0:n], ACT.Exp).then_inc(exped, 1)

            def job(what, i):
                act.wait_ge(misc_made, turn[what.replace("copy", "turn"), i] + 1)
                dst = y_feat[:, :, :] if what == "y_copy" else h_feat[:, :, i * P:(i + 1) * P]
                act.activation(dst, ps[:, 7, 0:D].rearrange("p (c q) -> p c q", c=DC), ACT.Copy).then_inc(misc_used, 1)

            for u in range(STEPS):
                for i in act_first[u]:
                    act.wait_ge(summed, B_FIRST[i + 1] if i + 1 < TILES else NB)
                    if i:
                        act.wait_ge(misc_made, turn["o_turn", i - 1] + 1)
                    act.activation(o_sb[:, :, :].rearrange("p g q -> p (g q)"), ps[:, 6, :], ACT.Copy).then_inc(o_copied, 1)
                if u < NB:
                    exp(u)
                for what, i in act_at[u]:
                    job(what, i)
            act.wait_ge(top_ready, TILES)
            act.activation(top_e[:, :, :], top_d[:, :, :], ACT.Exp).then_inc(top_exped, 1)
            act.wait_ge(summed, NB)
            for n in range(4):
                chunk, inner = n // 2, n % 2
                act.wait_ge(shared_up, n + 1)
                act.activation(shared_sig[:, inner, chunk * 512:(chunk + 1) * 512], ps[:, 2 * (n % 3), :],
                               ACT.Silu).then_inc(shared_silu, 1)

            act.wait_ge(places_ready, 2)
            act.activation(block_row[:, 1, :, :], block_onehot[:, :, :], ACT.Copy, scale=partition[:, 0:1]).then_inc(places_scaled, 1)

            def step(b, n, r, q):
                if n < MAX_BLOCKS:
                    act.wait_ge(gate_up, b + 1)
                    act.activation(silu_sb[:, r, :], ps[:, n % 2, 0:P], ACT.Silu).then_inc(silu_ready, 1)
                if n + 1 < MAX_BLOCKS:
                    turn_x_copy(b + 1, n + 1, (r + 1) % RING)

            def turn_x_copy(b, n, r):
                act.wait_ge(xs_turned, b + 1)
                act.activation(xs_feat[:, r, :, :].rearrange("p c q -> p (c q)"), ps[:, 2 + n % 2, 0:D],
                               ACT.Copy).then_inc(xs_ready, 1)

            turn_x_copy(0, 0, 0)
            over_blocks(act, step)

        @block.vector
        def _(dve):
            steps = [0]

            def link(ins):
                steps[0] += 1
                ins.then_inc(dve_step, 1)
                dve.wait_ge(dve_step, steps[0])

            def note(ins):
                steps[0] += 1
                ins.then_inc(dve_step, 1)

            note(dve.memset(qk_tok[:, :, 0:HEADS, 0:2], 0.0))
            dve.memset(qk_tok[:, :, HEADS:2 * HEADS, 0:2], 1.0).then_inc(stack_consts, 1)
            for g in range(2):
                for j in range(4 * g, 4 * g + 4):
                    dve.wait_ge(x_loaded[j // 2], 16)
                    note(dve.bn_stats(stats[:, j, :], x_sb[:, j, :]))
                dve.wait_ge(dve_step, steps[0])
                for j in range(4 * g, 4 * g + 4):
                    note(dve.bn_aggr(mean_var[:, j, :], stats[:, j, :]))
                dve.wait_ge(dve_step, steps[0])
                dve.tensor_scalar(var_eps[:, 4 * g:4 * g + 4], mean_var[:, 4 * g:4 * g + 4, 1], EPS_LN, None,
                                  ALU.add).then_inc(stats_ready, 1)

            def normalise(j):
                dve.wait_ge(rstd_ready, j // 4 + 1)
                dve.tensor_scalar(xn[:, j, :], x_sb[:, j, :], mean_var[:, j, 0:1], rstd[:, j:j + 1],
                                  ALU.subtract, ALU.mult).then_inc(xn_ready, 1)

            normalise(0)
            normalise(1)
            for j in range(TILES + 1):
                if j + 2 < TILES:
                    normalise(j + 2)
                if j < TILES:
                    dve.wait_ge(a_ready, 2 * (j + 1))
                    if j >= 2:
                        dve.wait_ge(b_ready, j - 1)
                    for heads, scale in ((queries, QK_SCALE), (keys, 1.0)):
                        dve.scalar_tensor_tensor(out=rest[:, j % 2, heads, :],
                                                 in0=ps[:, 2 + j % 2, heads.start * HD:heads.stop * HD].rearrange(
                                                     "p (h d) -> p h d", d=HD), scalar=scale,
                                                 in1=qk_tok[:, j % 2, heads, 2 + HD:2 + 2 * HD],
                                                 op0=ALU.mult, op1=ALU.subtract).then_inc(rest_ready, 1)
                    dve.wait_ge(v_made, j + 1)
                    if j == 0:
                        dve.wait_ge(consts, 1)
                    dve.tensor_copy(v_ext[:, j, :, 0:HD],
                                    ps[:, 4 + j % 2, 0:D].rearrange("p (h d) -> p h d", h=HEADS)).then_inc(v_ready, 1)
                if j:
                    for g, dst in enumerate((q_stack, k_stack)):
                        dve.wait_ge(stacked[1], 2 * (j - 1) + g + 1)
                        dve.tensor_copy(dst[0:ROWS, 8:16, (j - 1) * P:j * P],
                                        ps[0:ROWS, 7, :].bitcast(BF16).rearrange("p (h q) -> p h q", h=8)
                                        ).then_inc(stack_ready[1], 1)
                if j < TILES:
                    dve.wait_ge(rest_ready, 2 * (j + 1))
                    dve.wait_ge(b_ready, j + 1)
                    b_at, at = 2 + 4 * HD, {0: 2 + 5 * HD, HEADS: 2}
                    for h in (0, HEADS):
                        dve.tensor_tensor(qk_tok[:, j % 2, h:h + HEADS, at[h]:at[h] + HD], rest[:, j % 2, h:h + HEADS, :],
                                          qk_tok[:, j % 2, h:h + HEADS, b_at:b_at + HD], ALU.subtract).then_inc(c_ready, 1)

            for g in range(2):
                dve.wait_ge(stack_ready[g], 2 * TILES)
            dve.memset(ps[:, 6, :], 0.0).then_inc(sums_cleared, 1)

            def maximum(a):
                i, heads, k0, kw, part, _ = A_UNITS[a]
                dve.wait_ge(rows_scored, a + 1)
                dve.tensor_reduce(row_max[:, part, i, heads[0]:heads[-1] + 1],
                                  ps[:, a % 2, 0:len(heads) * kw].rearrange("p (h k) -> p h k", h=len(heads)),
                                  X, ALU.max).then_inc(row_maxed, 1)

            def job(what, i):
                if what == "max_join":
                    dve.wait_ge(row_maxed, A_LAST[i] + 1)
                    dve.tensor_tensor(row_max[:, 0, i, :], row_max[:, 0, i, :], row_max[:, 1, i, :],
                                      ALU.max).then_inc(max_joined, 1)
                elif what == "max_copy":
                    dve.wait_ge(misc_made, turn["max_turn", i] + 1)
                    if i >= 2:
                        dve.wait_ge(max_placed[i % 2], 32 * (i // 2))
                    link(dve.tensor_scalar(neg_max[:, i % 2, 0, :], ps[0:HEADS, 7, 0:P], -1.0, None, ALU.mult))
                    dve.scalar_tensor_tensor(out=neg_max[:, i % 2, 1, :], in0=ps[0:HEADS, 7, 0:P], scalar=-1.0,
                                             in1=neg_max[:, i % 2, 0, :], op0=ALU.mult,
                                             op1=ALU.subtract).then_inc(misc_used, 1)
                elif what == "norm":
                    dve.wait_ge(misc_made, turn["o_turn", i] + 1)
                    sums = ps[:, 7, :].rearrange("p (h c) -> p h c", h=HEADS)
                    if i:
                        dve.wait_ge(misc_made, turn["y_turn", i - 1] + 1)
                    link(dve.reciprocal(denom[:, :], sums[:, :, HD]))
                    dve.tensor_tensor(y_tok[:, :].rearrange("p (h d) -> p h d", h=HEADS), sums[:, :, 0:HD],
                                      denom[:, :].unsqueeze(2).broadcast_to([P, HEADS, HD]), ALU.mult).then_inc(misc_used, 1)
                elif what == "residual":
                    dve.wait_ge(misc_made, turn["proj", i] + 1)
                    x_i = x_sb[:, i, :]
                    ins = dve.tensor_tensor(x_i, x_i, ps[:, 7, D:2 * D], ALU.add)
                    ins.then_inc(misc_used, 1)
                    dve.wait_ge(misc_used, turn["proj", i] + 1)
                    link(dve.bn_stats(stats2[:, :], x_i))
                    if i >= 2:
                        dve.wait_ge(base_ready, i - 1)
                    link(dve.bn_aggr(mean_var2[:, i % 2, :], stats2[:, :]))
                    var = mean_var2[:, i % 2, 1:2]
                    link(dve.tensor_scalar(var_args[:, i % 2, 0:1], var, EPS_LN, None, ALU.add))
                    dve.scalar_tensor_tensor(out=var_args[:, i % 2, 1:2], in0=var_args[:, i % 2, 0:1], scalar=EPS_RMS,
                                             in1=var, op0=ALU.mult, op1=ALU.add).then_inc(var_ready, 1)
                elif what == "h":
                    dve.wait_ge(rstd2_ready, i + 1)
                    link(dve.tensor_scalar(h_raw[:, :], x_sb[:, i, :], mean_var2[:, i % 2, 0:1], rstd2[:, i % 2, 1:2],
                                           ALU.subtract, ALU.mult))
                    if i == 0:
                        dve.wait_ge(nw_loaded, 16)
                    dve.tensor_tensor(h_tok[:, i, :], h_raw[:, :], nw_sb[:, :], ALU.mult).then_inc(h_ready, 1)
                    dve.wait_ge(h_ready, i + 1)
                elif what == "top":
                    dve.wait_ge(misc_made, turn["logits", i] + 1)
                    dve.tensor_copy(logit_sb[:, i, :], ps[:, 7, D:D + EXPERTS]).then_inc(misc_used, 1)
                    dve.wait_ge(misc_used, turn["logits", i] + 1)
                    link(dve.max(top_v[:, i, :], logit_sb[:, i, :]))
                    note(dve.max_index(top_i[:, i, :], top_v[:, i, :], logit_sb[:, i, :]))
                    dve.tensor_scalar(top_d[:, i, :], top_v[:, i, 0:TOPK], top_v[:, i, 0:1], None,
                                      ALU.subtract).then_inc(top_ready, 1)

            for a in range(A_LAST[0] + 1):
                maximum(a)
            job("max_copy", 0)
            for a in range(A_FIRST[1], A_LAST[1] + 1):
                maximum(a)
            for u in range(STEPS):
                for what, i in dve_at[u]:
                    job(what, i)
                if u < NB:
                    for a in a_at[u]:
                        maximum(a)

            dve.wait_ge(dve_step, steps[0])
            link(dve.tensor_copy(idx_f[:, :, :], top_i[:, :, 0:TOPK]))
            onehot_v = onehot[:, :, :, :].rearrange("p t k e -> p (t k) e")
            dve.wait_ge(summed, NB)
            link(dve.tensor_tensor(onehot_v, iota_e.unsqueeze(1).broadcast_to([P, TILES * TOPK, EXPERTS]),
                                   idx_f[:, :, :].rearrange("p t k -> p (t k)").unsqueeze(2).broadcast_to(
                                       [P, TILES * TOPK, EXPERTS]), ALU.is_equal))
            with nc.allow_low_precision(reason="a token chooses an expert once or not: 0 or 1"):
                dve.tensor_reduce(chosen[:, :, :], onehot[:, :, :, :].rearrange("p t k e -> p t e k"),
                                  X, ALU.add).then_inc(chosen_ready, 1)
            dve.wait_ge(ranked, 1)
            counts = ps[:, 6, 256:256 + EXPERTS]
            ranks = ps[:, 6, 0:TILES * EXPERTS].rearrange("p (t e) -> p t e", t=TILES)
            link(dve.tensor_scalar(count_i[:, 0, :], counts, float(P - 1), None, ALU.add))
            link(dve.tensor_scalar(count_i[:, 1, :], count_i[:, 0, :], 7, None, ALU.arith_shift_right))
            link(dve.tensor_copy(nblk[:, :], count_i[:, 1, :]))
            link(dve.tensor_tensor_scan(nblk_end[:, :], nblk[:, :], zeros[:, 0:EXPERTS], 0.0, ALU.add, ALU.add))
            link(dve.tensor_tensor(nblk_start[:, :], nblk_end[:, :], nblk[:, :], ALU.subtract))
            link(dve.scalar_tensor_tensor(out=slot_te[:, :, :],
                                          in0=nblk_start[:, :].unsqueeze(1).broadcast_to([P, TILES, EXPERTS]),
                                          scalar=float(P), in1=ranks, op0=ALU.mult, op1=ALU.add))
            link(dve.tensor_tensor(slot_of[:, :, :, :], onehot[:, :, :, :],
                                   slot_te[:, :, :].unsqueeze(2).broadcast_to([P, TILES, TOPK, EXPERTS]), ALU.mult))
            link(dve.tensor_reduce(slot_f[:, :], slot_of[:, :, :, :].rearrange("p t k e -> p (t k) e"), X, ALU.add))
            dve.tensor_copy(slot_i[:, :], slot_f[:, :]).then_inc(slots_ready, 1)

            def shared(n):
                chunk, inner = n // 2, n % 2
                cols = slice(chunk * 512, (chunk + 1) * 512)
                dve.wait_ge(shared_silu, n + 1)
                dve.tensor_tensor(shared_act[:, inner, cols], shared_sig[:, inner, cols], ps[:, 2 * (n % 3) + 1, :],
                                  ALU.mult).then_inc(shared_ready, 1)

            shared(0)
            dve.wait_ge(base_ready, TILES)
            link(dve.tensor_tensor(below[:, :, :], nblk_end[0:1, :].unsqueeze(1).broadcast_to([1, MAX_BLOCKS, EXPERTS]),
                                   iota_b.unsqueeze(2).broadcast_to([1, MAX_BLOCKS, EXPERTS]), ALU.is_le))
            link(dve.tensor_reduce(expert_f[:, :], below[:, :, :], X, ALU.add))
            link(dve.memset(w_off[:, :], 0))
            dve.tensor_scalar(w_off[:, OFF_PAD:OFF_PAD + MAX_BLOCKS], expert_f[:, :], float(EXPERTS - 1), float(D), ALU.min,
                              ALU.mult).then_inc(offsets_ready, 1)
            shared(1)
            link(dve.tensor_scalar(place[:, 0, :], slot_i[:, :], P - 1, None, ALU.bitwise_and))
            link(dve.tensor_scalar(place[:, 1, :], slot_i[:, :], 7, None, ALU.arith_shift_right))
            link(dve.tensor_copy(place_f[:, :, :], place[:, :, :]))
            pairs = TILES * TOPK
            dve.tensor_tensor(pos_onehot[:, :, :], iota_row[:, :].unsqueeze(1).broadcast_to([P, pairs, P]),
                              place_f[:, 0, :].unsqueeze(2).broadcast_to([P, pairs, P]),
                              ALU.is_equal).then_inc(places_ready, 1)
            shared(2)
            dve.tensor_tensor(block_onehot[:, :, :],
                              iota_row[:, 0:MAX_BLOCKS].unsqueeze(1).broadcast_to([P, pairs, MAX_BLOCKS]),
                              place_f[:, 1, :].unsqueeze(2).broadcast_to([P, pairs, MAX_BLOCKS]),
                              ALU.is_equal).then_inc(places_ready, 1)
            shared(3)
            dve.wait_ge(places_ready, 2)
            dve.tensor_tensor(block_row[:, 0, :, :], block_onehot[:, :, :],
                              row_base[:, :].unsqueeze(2).broadcast_to([P, pairs, MAX_BLOCKS]),
                              ALU.mult).then_inc(places_ready, 1)
            dve.wait_ge(top_exped, 1)
            link(dve.tensor_reduce(top_sum[:, :], top_e[:, :, :], X, ALU.add))
            link(dve.reciprocal(top_sum[:, :], top_sum[:, :]))
            note(dve.tensor_tensor(top_w[:, :, :], top_e[:, :, :],
                                   top_sum[:, :].unsqueeze(2).broadcast_to([P, TILES, TOPK]), ALU.mult))
            for t in range(TILES):
                dve.wait_ge(shared_down, t + 1)
                dve.wait_ge(base_ready, t + 1)
                dve.tensor_tensor(base[:, t, :], base[:, t, :], ps[:, 6 + t % 2, 0:D],
                                  ALU.add).then_inc(shared_added, 1)

            dve.wait_ge(rows_found, 1)
            table = ps[:, 4, 0:MAX_BLOCKS]
            link(dve.scalar_tensor_tensor(out=unused[:, :], in0=table, scalar=float(P), in1=spare_row[:, :],
                                          op0=ALU.is_lt, op1=ALU.mult))
            dve.scalar_tensor_tensor(out=row_i[:, :], in0=table, scalar=-float(P), in1=unused[:, :],
                                     op0=ALU.add, op1=ALU.add).then_inc(rows_ready, 1)

            def step(b, n, r, q):
                if 1 <= n <= MAX_BLOCKS:
                    dve.wait_ge(act_turned, b)
                    dve.tensor_copy(act_feat[:, (r - 1) % RING, :], ps[:, 4 + (n - 1) % 2, 0:P]).then_inc(act_feat_ready, 1)
                if n < MAX_BLOCKS:
                    dve.wait_ge(silu_ready, b + 1)
                    dve.tensor_tensor(act_sb[:, r, :], silu_sb[:, r, :], ps[:, n % 2, P:2 * P], ALU.mult).then_inc(act_ready, 1)
                if n >= 2:
                    r2 = (r - 2) % RING
                    dve.wait_ge(down, b - 1)
                    if n - 2 >= RING:
                        dve.wait_ge(ys_stored[r2], 16 * (q if r >= 2 else q - 1))
                    dve.tensor_copy(ys_sb[:, r2, :], ps[:, 6 + n % 2, 0:D]).then_inc(ys_ready, 1)

            over_blocks(dve, step)

            for t in range(TILES):
                dve.wait_ge(row_gathered[t], 16)
                for k in range(TOPK):
                    ins = dve.scalar_tensor_tensor(out=base[:, t, :], in0=gathered[:, TOPK * t + k, :],
                                                   scalar=top_w[:, t, k:k + 1], in1=base[:, t, :],
                                                   op0=ALU.mult, op1=ALU.add)
                    if k < TOPK - 1:
                        link(ins)
                    else:
                        ins.then_inc(combined, 1)


_INS = ["L0_attn_x", "L0_attn_w_attn", "L0_attn_w_proj", "L0_ffn_norm_w", "L0_ffn_router_w", "L0_ffn_w1",
        "L0_ffn_w2", "L0_ffn_sg", "L0_ffn_su", "L0_ffn_sd"]


def kernel(**inputs):
    import numpy as _np
    import concourse.bacc as _bacc
    from concourse import mybir as _mybir
    from concourse.bass_utils import run_bass_kernel_spmd as _run

    nc = _bacc.Bacc("TRN2", target_bir_lowering=False, num_devices=1)
    arrays, args = {}, []
    for name in _INS:
        a = _np.ascontiguousarray(inputs[name])
        arrays[f"in_{name}"] = a
        args.append(nc.dram_tensor(f"in_{name}", a.shape, _mybir.dt.from_np(a.dtype), kind="ExternalInput").ap())
    args.append(nc.dram_tensor("out_x", (1, T, D), F32, kind="ExternalOutput").ap())
    layer(nc, *args)
    r = _run(nc, [arrays], core_ids=[0])
    return r.results[0]["out_x"]
```

```python
from contextlib import ExitStack

import concourse.bass as bass
from concourse import mybir

F32 = mybir.dt.float32
BF16 = mybir.dt.bfloat16
I32 = mybir.dt.int32
U32 = mybir.dt.uint32
ALU = mybir.AluOpType
ACT = mybir.ActivationFunctionType
X = mybir.AxisListType.X

P = 128
T, D = 1024, 256
TILES = T // P
DC = D // P
HEADS, HD = 16, 16
QK_SCALE = HD ** -0.5
PARTS = 6
ROWS = 2 + PARTS * HD
VW = HD + 1
EXPERTS, TOPK = 32, 4
MAX_BLOCKS = (T * TOPK + EXPERTS * (P - 1)) // P
SLOTS = MAX_BLOCKS * P
REGION = T + P
ZERO_ROW = EXPERTS * REGION
PAD_TILE = TILES - 2
RING = 4
TABLE_STEP = 2
OFF_PAD = 5
MAX_LEAD = 6
P_RING = 4
EPS_LN, EPS_RMS = 1e-5, 1e-6
NEG = -1e30


def max_units():
    units, first, last = [], [], []
    for i in range(TILES):
        first.append(len(units))
        width = (i + 1) * P
        w0 = min(width, 512)
        per = 512 // w0
        for a in range(0, HEADS, per):
            units.append((i, list(range(a, a + per)), 0, w0, 0, width <= 512))
        if width > 512:
            w1 = width - 512
            per = 512 // w1
            for a in range(0, HEADS, per):
                units.append((i, list(range(a, a + per)), 512, w1, 1, True))
        last.append(len(units) - 1)
    return units, first, last


def prob_units():
    units, first = [], []
    for i in range(TILES):
        first.append(len(units))
        per = 2 if i < 4 else 1
        for h in range(0, HEADS, per):
            units.append((i, list(range(h, h + per))))
    return units, first


def layer(nc, x, w_attn, w_proj, norm_w, router_w, w1, w2, sg, su, sd, out):
    A_UNITS, A_FIRST, A_LAST = max_units()
    B_UNITS, B_FIRST = prob_units()
    NB = len(B_UNITS)
    STEPS = NB + 10

    a_at = [[] for _ in range(STEPS)]
    pe_at = [[] for _ in range(STEPS)]
    dve_at = [[] for _ in range(STEPS)]
    act_at = [[] for _ in range(STEPS)]
    act_first = [[] for _ in range(STEPS)]
    pool_at = [[] for _ in range(STEPS)]
    early = {(j, point): [] for j in range(TILES + 1) for point in range(4)}
    for j in range(2, TILES):
        early[j, 0].append(2 * (j - 2))
        early[j, 2].append(2 * (j - 2) + 1)
    EARLY = 2 * (TILES - 2)
    for n in range(4):
        early[TILES, 2 + n // 2].append(EARLY + n)
    EARLY += 4
    assert all(A_UNITS[a][0] <= j - 2 for (j, _), todo in early.items() for a in todo)
    end_at = {3: 8, 4: 18, 5: 32, 6: 52, 7: 74}
    begin = 0
    for i in range(3, TILES):
        assert end_at[i] <= B_FIRST[i] - MAX_LEAD
        todo = range(A_FIRST[i], A_LAST[i] + 1)
        for a, unit in enumerate(todo):
            a_at[begin + a * (end_at[i] - begin) // len(todo)].append(unit)
        begin = end_at[i]
    for i in range(TILES):
        s = (B_FIRST[i + 1] if i + 1 < TILES else NB) + 1
        spread = 3 <= i < TILES - 1
        y, proj, norm, h, h_turn, logits, rank = (2, 4, 6, 8, 9, 11, 13) if spread else (1, 2, 3, 4, 4, 5, 7)
        if i == PAD_TILE:
            y, proj, norm, h, h_turn, logits, rank = 1, 3, 4, 5, 6, 7, 9
        act_first[s].append(i)
        pe_at[s].append(("o_turn", i))
        dve_at[s + 1].append(("norm", i))
        pe_at[s + y].append(("y_turn", i))
        act_at[s + y + 1].append(("y_copy", i))
        pe_at[s + proj].append(("proj", i))
        dve_at[s + proj + 1].append(("residual", i))
        pool_at[s + norm].append(("rstd", i))
        act_at[s + h].append(("h_raw", i))
        dve_at[s + h].append(("h", i))
        act_at[s + h_turn].append(("base", i))
        pe_at[s + h_turn].append(("h_turn", i))
        act_at[s + h_turn + 1].append(("h_copy", i))
        pe_at[s + logits].append(("logits", i))
        dve_at[s + logits + 1].append(("top", i))
        pe_at[s + rank].append(("rank", i))
        dve_at[s + rank + 1].append(("slot", i))
        for k in range(TOPK):
            pool_at[min(s + rank + 1 + k * (1 if i == TILES - 1 else 2), STEPS - 1)].append(("scatter", TOPK * i + k))
        if i:
            s = B_FIRST[i] - MAX_LEAD + 1
            if i >= 4:
                dve_at[s].append(("max_join", i))
            pe_at[s].append(("max_turn", i))
            dve_at[s + 1].append(("max_copy", i))

    order = [("max_turn", 0)] + [job for jobs in pe_at for job in jobs]
    turn = {job: n for n, job in enumerate(order)}

    s = NB + 1
    pe_fill = {s: ("up", 0, 0), s + 1: ("up", 0, 1), s + 2: ("up", 1, 0), s + 3: ("up", 1, 1)}
    act_fill = {s + 3: 0, s + 5: 1}
    dve_fill = {s + 1: ("positions", 0, TILES // 2), s + 4: ("shared", 0), s + 6: ("shared", 1)}

    ctx = ExitStack()
    with ctx:
        start = nc.sbuf_base + (-nc.sbuf_base) % 64
        end = nc.sbuf_usable_end
        cursor = [start]

        def sb(name, shape, dt, at=None):
            size = int(mybir.dt.size(dt))
            for n in shape[1:]:
                size *= n
            if at is None:
                at = cursor[0]
                cursor[0] += size + (-size) % 64
                assert cursor[0] <= end, (name, cursor[0], end)
            return nc.alloc_sbuf_tensor_at(name, shape, dt, offset=at)

        KB = 1024
        w1_at = cursor[0]
        w1_sb = sb("w1_sb", [P, EXPERTS * DC * D], F32)
        gathered = sb("gathered", [P, TILES * TOPK, D], F32, w1_at)
        q_at = cursor[0]
        q_stack = sb("q_stack", [P, TILES, HEADS, P], BF16)
        w2_sb = sb("w2_sb", [P, EXPERTS * D], F32, q_at)
        k_at = cursor[0]
        k_stack = sb("k_stack", [P, HEADS, T], BF16)
        shared_sig = sb("shared_sig", [P, 2, T], F32, k_at)
        shared_act = sb("shared_act", [P, 2, T], F32, k_at + 8 * KB)
        ys_sb = sb("ys_sb", [P, RING, D], F32, k_at)
        silu_sb = sb("silu_sb", [P, RING, P], F32, k_at + 4 * KB)
        xs_tok = sb("xs_tok", [P, RING, D], F32, k_at + 16 * KB)
        xs_feat = sb("xs_feat", [P, RING, DC, P], F32, k_at + 20 * KB)
        act_sb = sb("act_sb", [P, RING, P], F32, k_at + 24 * KB)
        act_feat = sb("act_feat", [P, RING, P], F32, k_at + 26 * KB)
        v_ext = sb("v_ext", [P, TILES, HEADS, VW], F32)
        x_sb = sb("x_sb", [P, TILES, D], F32)
        tok_at = cursor[0]
        xn = sb("xn", [P, TILES, D], F32)
        h_tok = sb("h_tok", [P, TILES, D], F32, tok_at)
        base = x_sb
        feat_at = cursor[0]
        xn_feat = sb("xn_feat", [P, DC, T], F32)
        h_feat = sb("h_feat", [P, DC, T], F32, feat_at)
        st_at = cursor[0]
        qk_tok = sb("qk_tok", [P, 2, 2 * HEADS, ROWS], BF16)
        rest = sb("rest", [P, 2, 2 * HEADS, HD], F32)
        probs = sb("probs", [P, P_RING, T], F32, st_at)
        pair_start = sb("pair_start", [P, TILES * TOPK, EXPERTS], F32, st_at + 8 * KB)
        pos_onehot = sb("pos_onehot", [P, TILES * TOPK, P], BF16, st_at)
        block_onehot = sb("block_onehot", [P, TILES * TOPK, MAX_BLOCKS], BF16, st_at + 8 * KB)
        block_row = sb("block_row", [P, 2, TILES * TOPK, MAX_BLOCKS], BF16, feat_at)
        wa_at = cursor[0]
        wa_sb = sb("wa_sb", [P, DC, 3 * D], F32)
        onehot = sb("onehot", [P, TILES, TOPK, EXPERTS], F32, wa_at)
        logit_sb = sb("logit_sb", [P, TILES, EXPERTS], F32, wa_at + 4 * KB)
        chosen = sb("chosen", [P, TILES, EXPERTS], BF16, wa_at + 5 * KB)
        top_v = sb("top_v", [P, TILES, 8], F32, wa_at + 5 * KB + 512)
        top_i = sb("top_i", [P, TILES, 8], U32, wa_at + 5 * KB + 768)
        wp_sb = sb("wp_sb", [P, DC, D], F32)
        sg_sb = sb("sg_sb", [P, DC, D], F32)
        su_sb = sb("su_sb", [P, DC, D], F32)
        sd_sb = sb("sd_sb", [P, DC, D], F32)
        nw_sb = sb("nw_sb", [P, D], F32)
        zeros = sb("zeros", [P, D], F32)
        ident = sb("ident", [P, P], F32)
        ident_b = sb("ident_b", [P, P], BF16)
        before_b = sb("before_b", [P, P], BF16)
        ones_b = sb("ones_b", [P, P], BF16)
        future_b = sb("future_b", [P, P], BF16)
        router_at = cursor[0]
        router_sb = sb("router_sb", [EXPERTS, D], F32)
        slot_of = sb("slot_of", [P, TOPK, EXPERTS], F32, router_at)
        slot_te = sb("slot_te", [P, EXPERTS], F32, router_at + 512)
        slot_f = sb("slot_f", [P, TILES, TOPK], F32, router_at + 640)
        idx_f = sb("idx_f", [P, TILES, TOPK], F32, router_at + 768)
        pad_i = sb("pad_i", [1, EXPERTS], I32, router_at + 896)
        router_feat = sb("router_feat", [P, DC, EXPERTS], F32)
        powers = sb("powers", [P, 16], F32)
        iota_row = sb("iota_row", [P, P], F32)
        iota_e, iota_b = iota_row[:, 0:EXPERTS], iota_row[0:1, 0:MAX_BLOCKS]
        partition = sb("partition", [P, 1], F32)
        spare_row = sb("spare_row", [P, MAX_BLOCKS], F32)
        row_base = sb("row_base", [P, TILES * TOPK], F32)
        stats = sb("stats", [P, TILES, 6], F32)
        mean_var = sb("mean_var", [P, TILES, 2], F32)
        var_eps = sb("var_eps", [P, TILES], F32)
        rstd = sb("rstd", [P, TILES], F32)
        row_max = sb("row_max", [P, 2, TILES, HEADS], F32)
        neg_max = sb("neg_max", [HEADS, 2, 2, P], BF16)
        denom = sb("denom", [P, HEADS], F32)
        o_sb = sb("o_sb", [P, 4, P], F32)
        y_tok = sb("y_tok", [P, D], F32)
        y_feat = sb("y_feat", [P, DC, P], F32)
        stats2 = sb("stats2", [P, 6], F32)
        mean_var2 = sb("mean_var2", [P, 2, 2], F32)
        var_args = sb("var_args", [P, 2, 2], F32)
        rstd2 = sb("rstd2", [P, 2, 2], F32)
        h_raw = sb("h_raw", [P, D], F32)
        shift2 = sb("shift2", [P, 2, 2], F32)
        scale_base = sb("scale_base", [P, 2, 1], F32)
        top_d = sb("top_d", [P, TILES, TOPK], F32)
        top_e = sb("top_e", [P, TILES, TOPK], F32)
        top_sum = sb("top_sum", [P, TILES], F32)
        top_w = sb("top_w", [P, TILES, TOPK], F32)
        small_at = [k_at + 28 * KB]

        def small(name, shape, dt):
            at = small_at[0]
            small_at[0] += shape[1] * 4 + (-shape[1] * 4) % 64
            assert small_at[0] <= k_at + 32 * KB
            return sb(name, shape, dt, at)

        count_i = small("count_i", [P, 2 * EXPERTS], I32)
        nblk, nblk_end = small("nblk", [P, EXPERTS], F32), small("nblk_end", [P, EXPERTS], F32)
        nblk_start = small("nblk_start", [P, EXPERTS], F32)
        below, below_rows = small("below", [P, EXPERTS], F32), small("below_rows", [P, EXPERTS], F32)
        rows_less = small("rows_less", [P, EXPERTS], F32)
        block_cols = small("block_cols", [P, 4], F32)
        w_off = small("w_off", [1, OFF_PAD + MAX_BLOCKS + RING], I32)
        x_row = small("x_row", [1, 1 + MAX_BLOCKS + 2 * RING], I32)
        place = small("place", [P, 2 * TILES * TOPK], I32)
        place_f = small("place_f", [P, 2 * TILES * TOPK], F32)
        pair_first = small("pair_first", [P, TILES * TOPK], F32)
        unused = small("unused", [P, MAX_BLOCKS], F32)
        region_base = sb("region_base", [P, EXPERTS], F32)
        slot_i = sb("slot_i", [P, TILES * TOPK], I32)
        row_i = sb("row_i", [P, MAX_BLOCKS], I32)

        xs_dram = nc.dram_tensor("xs_dram", [ZERO_ROW + P, D], F32).ap()
        pair_dram = nc.dram_tensor("pair_dram", [T * TOPK + SLOTS, D], F32).ap()

        ps = ctx.enter_context(nc.psum_tensor("ps", [P, 8, 512], F32))

        def sem(name):
            return ctx.enter_context(nc.semaphore(name))

        x_loaded = [sem(f"x_loaded{n}") for n in range(4)]
        wa_loaded, wp_loaded, router_loaded = sem("wa_loaded"), sem("wp_loaded"), sem("router_loaded")
        nw_loaded, shared_loaded = sem("nw_loaded"), sem("shared_loaded")
        w1_loaded, w2_loaded, xs_cleared = sem("w1_loaded"), sem("w2_loaded"), sem("xs_cleared")
        zeros_ready, consts, stack_consts = sem("zeros_ready"), sem("consts"), sem("stack_consts")
        pool_step, dve_step = sem("pool_step"), sem("dve_step")
        stats_ready, rstd_ready, xn_ready = sem("stats_ready"), sem("rstd_ready"), sem("xn_ready")
        router_turned, router_ready = sem("router_turned"), sem("router_ready")
        xn_turned, xn_feat_ready = sem("xn_turned"), sem("xn_feat_ready")
        qk_made, v_made = sem("qk_made"), sem("v_made")
        a_ready, rest_ready = sem("a_ready"), sem("rest_ready")
        b_ready, c_ready, copies_ready, v_ready = sem("b_ready"), sem("c_ready"), sem("copies_ready"), sem("v_ready")
        stacked = [sem("stacked0"), sem("stacked1")]
        stack_ready = [sem("stack_ready_act"), sem("stack_ready_dve")]
        rows_scored, row_maxed, max_joined = sem("rows_scored"), sem("row_maxed"), sem("max_joined")
        max_placed = [sem("max_placed0"), sem("max_placed1")]
        scored, exped, masked, summed = sem("scored"), sem("exped"), sem("masked"), sem("summed")
        sums_cleared, o_copied = sem("sums_cleared"), sem("o_copied")
        misc_made, misc_used = sem("misc_made"), sem("misc_used")
        var_ready, rstd2_ready, norm_ready = sem("var_ready"), sem("rstd2_ready"), sem("norm_ready")
        h_raw_ready, h_ready = sem("h_raw_ready"), sem("h_ready")
        base_ready, top_ready, top_exped = sem("base_ready"), sem("top_ready"), sem("top_exped")
        chosen_ready, slots_ready = sem("chosen_ready"), sem("slots_ready")
        offsets_ready, positions_ready, blocks_ready = sem("offsets_ready"), sem("positions_ready"), sem("blocks_ready")
        places_scaled = [sem("rows_scaled"), sem("places_scaled")]
        rows_found, rows_ready = sem("rows_found"), sem("rows_ready")
        shared_up, shared_silu, shared_ready = sem("shared_up"), sem("shared_silu"), sem("shared_ready")
        shared_down, shared_added = sem("shared_down"), sem("shared_added")
        scattered, pads_ready, padded = sem("scattered"), sem("pads_ready"), sem("padded")
        cols_ready, cols_turned = sem("cols_ready"), sem("cols_turned")
        xs_loaded = [sem(f"xs_loaded{r}") for r in range(RING)]
        ys_stored = [sem(f"ys_stored{r}") for r in range(RING)]
        xs_turned, xs_ready, gate_up = sem("xs_turned"), sem("xs_ready"), sem("gate_up")
        silu_ready, act_ready, act_turned = sem("silu_ready"), sem("act_ready"), sem("act_turned")
        act_feat_ready, down, ys_ready = sem("act_feat_ready"), sem("down"), sem("ys_ready")
        row_gathered = [sem(f"row_gathered{t}") for t in range(TILES)]
        combined, stored = sem("combined"), sem("stored")

        x_d = x.rearrange("a (t p) d -> p (a t) d", p=P)
        out_d = out.rearrange("a (t p) d -> p (a t) d", p=P)

        def part(j, heads, n, count=1, step=1):
            v = qk_tok[:, j % 2, heads, 2:ROWS].rearrange("p h (s d) -> p h s d", s=PARTS)
            return v[:, :, n:n + (count - 1) * step + 1:step, :]

        queries, keys = slice(0, HEADS), slice(HEADS, 2 * HEADS)

        def over_blocks(engine, step):
            head = 2 * RING - 1
            turns = (MAX_BLOCKS - RING - head) // RING
            for b in range(head):
                step(b, b, b % RING, b // RING)
            with engine.Fori(0, turns) as it:
                for n in range(head, head + RING):
                    step(it * RING + n, n, n % RING, it + n // RING)
            for b in range(head + turns * RING, MAX_BLOCKS + 2):
                step(b, b, b % RING, b // RING)

        block = ctx.enter_context(nc.Block())

        @block.sync
        def _(sp):
            for n in range(4):
                sp.dma_start(x_sb[:, 2 * n:2 * n + 2, :], x_d[:, 2 * n:2 * n + 2, :]).then_inc(x_loaded[n], 16)
            sp.dma_start(router_sb[:, :], router_w).then_inc(router_loaded, 16)
            sp.dma_start(wa_sb[:, :, :], w_attn.rearrange("(c p) n -> p c n", p=P)).then_inc(wa_loaded, 16)
            sp.dma_start(wp_sb[:, :, :], w_proj.rearrange("(c p) n -> p c n", p=P)).then_inc(wp_loaded, 16)
            sp.dma_start(nw_sb[:, :], norm_w.rearrange("(a n) -> a n", a=1).broadcast_to([P, D])).then_inc(nw_loaded, 16)
            for dst, src in ((sg_sb, sg), (su_sb, su), (sd_sb, sd)):
                sp.dma_start(dst[:, :, :], src.rearrange("(c p) n -> p c n", p=P)).then_inc(shared_loaded, 16)
            sp.wait_ge(zeros_ready, 1)
            sp.dma_start(xs_dram[ZERO_ROW:ZERO_ROW + P, :], zeros[:, :]).then_inc(xs_cleared, 16)
            w1_v = w1_sb[:, :].rearrange("p (c e n) -> p c e n", e=EXPERTS, c=DC)
            for c in range(DC):
                sp.dma_start(w1_v[:, c, :, :], w1[:, c * P:(c + 1) * P, :].rearrange("e p n -> p e n")).then_inc(w1_loaded, 16)
            per = EXPERTS // TILES

            def load_w2(i):
                sp.wait_ge(scored, B_FIRST[i + 1] if i + 1 < TILES else NB)
                sp.dma_start(w2_sb[:, i * per * D:(i + 1) * per * D].rearrange("p (e n) -> p e n", e=per),
                             w2[i * per:(i + 1) * per, :, :].rearrange("e p n -> p e n")).then_inc(w2_loaded, 16)

            for i in range(TILES):
                sp.wait_ge(misc_used, turn["max_turn", i] + 1)
                sp.wait_ge(rows_scored, A_LAST[i] + 1)
                for part in range(2):
                    sp.dma_start(q_stack[part:part + 1, i, :, :],
                                 neg_max[:, i % 2, part, :]).then_inc(max_placed[i % 2], 16)
                if i >= 2:
                    load_w2(i - 2)
            load_w2(TILES - 2)
            sp.wait_ge(pads_ready, 1)
            pads = [sp.alloc_register(f"pad{n}") for n in range(8)]
            for g in range(0, EXPERTS, 8):
                sp.load(pads, pad_i[0:1, g:g + 8])
                for n in range(8):
                    row = sp.snap(pads[n], min_val=0, max_val=ZERO_ROW - 2 * P)
                    sp.dma_start(xs_dram[bass.ds(row, 2 * P), :].rearrange("(k p) d -> p k d", p=P),
                                 zeros[:, :].unsqueeze(1).broadcast_to([P, 2, D])).then_inc(padded, 16)
            load_w2(TILES - 1)

            rows = [sp.alloc_register(f"row{n}") for n in range(RING)]

            def group(b):
                sp.load(rows, x_row[0:1, bass.ds(b + RING + 1, RING)])

            def load(r, n):
                row = sp.snap(rows[n], min_val=0, max_val=ZERO_ROW)
                sp.dma_start(xs_tok[:, r, :], xs_dram[bass.ds(row, P), :]).then_inc(xs_loaded[r], 16)

            sp.wait_ge(offsets_ready, 2)
            sp.wait_ge(xs_cleared, 16)
            sp.wait_ge(scattered, 16 * TILES * TOPK)
            group(-RING - 1)
            for b in range(RING - 1):
                load(b, b + 1)
            group(-1)
            load(RING - 1, 0)

            def step(b, n, r, q):
                g = (r + 1) % RING
                if g == 0:
                    group(b)
                if n + RING < MAX_BLOCKS:
                    sp.wait_ge(xs_turned, b + 1)
                    load(r, g)

            over_blocks(sp, step)
            for r in range(RING):
                sp.wait_ge(ys_stored[r], 16 * len(range(r, MAX_BLOCKS, RING)))
            for t in range(TILES):
                sp.dma_start(gathered[:, TOPK * t:TOPK * (t + 1), :],
                             pair_dram[TOPK * t * P:TOPK * (t + 1) * P, :].rearrange("(k p) d -> p k d", p=P)
                             ).then_inc(row_gathered[t], 16)
            for t in range(TILES):
                sp.wait_ge(combined, t + 1)
                sp.dma_start(out_d[:, t, :], base[:, t, :]).then_inc(stored, 16)
            sp.wait_ge(stored, 16 * TILES)

        @block.gpsimd
        def _(pool):
            steps = [0]

            def link(ins):
                steps[0] += 1
                ins.then_inc(pool_step, 1)
                pool.wait_ge(pool_step, steps[0])

            pool.memset(zeros[:, :], 0.0).then_inc(zeros_ready, 1)
            pool.memset(powers[:, :], -0.5)
            pool.memset(ones_b[:, :], 1.0)
            link(pool.memset(ident[:, :], 0.0))
            link(pool.affine_select(out=ident[:, :], in_=ident[:, :], compare_op=ALU.not_equal, fill=1.0, base=0,
                                    pattern=[[-1, P]], channel_multiplier=1))
            pool.tensor_copy(ident_b[:, :], ident[:, :])
            link(pool.memset(future_b[:, :], 0.0))
            pool.affine_select(out=future_b[:, :], in_=future_b[:, :], compare_op=ALU.is_ge, fill=NEG, base=0,
                               pattern=[[-1, P]], channel_multiplier=1)
            pool.affine_select(out=before_b[:, :], in_=ones_b[:, :], compare_op=ALU.is_gt, fill=0.0, base=0,
                               pattern=[[1, P]], channel_multiplier=-1)
            pool.iota(iota_row[:, :], [[1, P]], base=0, channel_multiplier=0, allow_small_or_imprecise_dtypes=True)
            pool.iota(partition[:, :], [[0, 1]], base=0, channel_multiplier=1, allow_small_or_imprecise_dtypes=True)
            pool.iota(spare_row[:, :], [[P, MAX_BLOCKS]], base=T * TOPK + P, channel_multiplier=1,
                      allow_small_or_imprecise_dtypes=True)
            pool.iota(region_base[:, :], [[REGION, EXPERTS]], base=0, channel_multiplier=0,
                      allow_small_or_imprecise_dtypes=True)
            link(pool.iota(row_base[:, :], [[P, TILES * TOPK]], base=P, channel_multiplier=0,
                           allow_small_or_imprecise_dtypes=True))
            pool.memset(v_ext[:, :, :, HD:VW], 1.0).then_inc(consts, 1)
            for g in range(2):
                pool.wait_ge(stats_ready, g + 1)
                pool.tensor_tensor(rstd[:, 4 * g:4 * g + 4], var_eps[:, 4 * g:4 * g + 4], powers[:, 0:4],
                                   ALU.pow).then_inc(rstd_ready, 1)

            both = slice(0, 2 * HEADS)
            for j in range(TILES):
                pool.wait_ge(rest_ready, 2 * (j + 1))
                pool.tensor_copy(part(j, both, 4), rest[:, j % 2, :, :].unsqueeze(2)).then_inc(b_ready, 1)
                pool.wait_ge(b_ready, j + 1)
                pool.tensor_copy(part(j, queries, 3), part(j, queries, 4))
                pool.tensor_copy(part(j, keys, 2), part(j, keys, 4)).then_inc(copies_ready, 1)

            def mask(u):
                i, heads = B_UNITS[u]
                pool.wait_ge(exped, u + 1)
                v = probs[:, u % P_RING, :].rearrange("p (a q) -> p a q", a=2 if len(heads) == 2 else 1)
                v = v[:, :, i * P:(i + 1) * P]
                pool.affine_select(out=v, in_=v, compare_op=ALU.is_ge, fill=0.0, base=0,
                                   pattern=[[0, len(heads)], [1, P]], channel_multiplier=-1).then_inc(masked, 1)

            for u in range(STEPS):
                if u < NB:
                    mask(u)
                for what, i in pool_at[u]:
                    if what == "scatter":
                        pool.wait_ge(slots_ready, i // TOPK + 1)
                        if i // TOPK > PAD_TILE:
                            pool.wait_ge(padded, 16 * EXPERTS)
                        pool.indirect_dma_start(xs_dram, bass.IndirectOffsetOnAxis(slot_i[:, i:i + 1], 0),
                                                h_tok[:, i // TOPK, :], None).then_inc(scattered, 16)
                        continue
                    pool.wait_ge(var_ready, i + 1)
                    pool.tensor_tensor(rstd2[:, i % 2, :], var_args[:, i % 2, :], powers[:, 0:2],
                                       ALU.pow).then_inc(rstd2_ready, 1)
                    pool.wait_ge(rstd2_ready, i + 1)
                    pool.tensor_scalar(shift2[:, i % 2, :], rstd2[:, i % 2, :], mean_var2[:, i % 2, 0:1], -1.0,
                                       ALU.mult, ALU.mult)
                    pool.tensor_scalar(scale_base[:, i % 2, :], rstd2[:, i % 2, 0:1], 1.0, None,
                                       ALU.add).then_inc(norm_ready, 1)

            pool.wait_ge(blocks_ready, 2)
            pool.wait_ge(shared_up, 4)
            pool.tensor_tensor(block_row[:, 0, :, :], block_onehot[:, :, :],
                               row_base[:, :].unsqueeze(2).broadcast_to([P, TILES * TOPK, MAX_BLOCKS]),
                               ALU.mult).then_inc(places_scaled[0], 1)
            pool.wait_ge(rows_ready, 1)
            for b in range(MAX_BLOCKS):
                pool.wait_ge(ys_ready, b + 1)
                pool.indirect_dma_start(pair_dram, bass.IndirectOffsetOnAxis(row_i[:, b:b + 1], 0),
                                        ys_sb[:, b % RING, :], None).then_inc(ys_stored[b % RING], 16)

        @block.tensor
        def _(pe):
            pe.wait_ge(consts, 1)
            pe.wait_ge(router_loaded, 16)
            for c in range(DC):
                last = pe.transpose(ps[:, 7, c * EXPERTS:(c + 1) * EXPERTS], router_sb[:, c * P:(c + 1) * P],
                                    ident[0:EXPERTS, 0:EXPERTS])
            last.then_inc(router_turned, 1)

            def turn_xn(j):
                pe.wait_ge(xn_ready, j + 1)
                if j:
                    pe.wait_ge(xn_feat_ready, j)
                for c in range(DC):
                    last = pe.transpose(ps[:, 0, c * P:(c + 1) * P], xn[:, j, c * P:(c + 1) * P], ident[:, :])
                last.then_inc(xn_turned, 1)

            def project(j):
                pe.wait_ge(xn_feat_ready, j + 1)
                if j >= 2:
                    pe.wait_ge(rest_ready, 2 * (j - 1))
                    pe.wait_ge(v_ready, j - 1)
                for c in range(DC):
                    last = pe.matmul(ps[:, 2 + j % 2, :], xn_feat[:, c, j * P:(j + 1) * P], wa_sb[:, c, 0:2 * D],
                                     start=(c == 0), stop=(c == DC - 1))
                last.then_inc(qk_made, 1)
                for c in range(DC):
                    last = pe.matmul(ps[:, 4 + j % 2, 0:D], xn_feat[:, c, j * P:(j + 1) * P], wa_sb[:, c, 2 * D:3 * D],
                                     start=(c == 0), stop=(c == DC - 1))
                last.then_inc(v_made, 1)

            def score_rows(a):
                i, heads, k0, kw, part, diagonal = A_UNITS[a]
                if a:
                    pe.wait_ge(row_maxed, a if a < EARLY else a - 1)
                bank = 1 if a < EARLY else a % 2
                for n, h in enumerate(heads):
                    last = pe.matmul(ps[:, bank, n * kw:(n + 1) * kw], q_stack[0:ROWS, i, h, :],
                                     k_stack[0:ROWS, h, k0:k0 + kw], start=True, stop=not diagonal)
                    if diagonal:
                        last = pe.matmul(ps[:, bank, (n + 1) * kw - P:(n + 1) * kw], ident_b[:, :], future_b[:, :],
                                         start=False, stop=True)
                last.then_inc(rows_scored, 1)

            def early_rows(j, point):
                for a in early[j, point]:
                    for g in range(2):
                        pe.wait_ge(stack_ready[g], 2 * A_UNITS[a][0] + 2)
                    score_rows(a)

            def stack(j):
                pe.wait_ge(copies_ready, j + 1)
                pe.wait_ge(c_ready, 2 * (j + 1))
                for g in range(4):
                    n = 2 * j + g // 2
                    if n:
                        pe.wait_ge(stack_ready[g % 2], n)
                    bank = ps[0:ROWS, 6 + g % 2, :].bitcast(BF16)
                    for h in range(8):
                        last = pe.transpose(bank[:, h * P:(h + 1) * P], qk_tok[:, j % 2, 8 * g + h, :], ident_b[:, :])
                    last.then_inc(stacked[g % 2], 1)
                    if g % 2:
                        early_rows(j + 1, 2 + g // 2)

            turn_xn(0)
            pe.wait_ge(wa_loaded, 16)
            pe.wait_ge(router_ready, 1)
            for j in range(TILES):
                if j + 1 < TILES:
                    turn_xn(j + 1)
                early_rows(j, 0)
                project(j)
                early_rows(j, 1)
                if j:
                    stack(j - 1)
            stack(TILES - 1)

            pe.wait_ge(xn_feat_ready, TILES)
            pe.wait_ge(v_ready, TILES)
            for g in range(2):
                pe.wait_ge(stack_ready[g], 2 * TILES)

            def turn_max(i):
                if i >= 4:
                    pe.wait_ge(max_joined, i - 3)
                else:
                    pe.wait_ge(row_maxed, A_LAST[i] + 1)
                return pe.transpose(ps[0:HEADS, 7, 0:P], row_max[:, 0, i, :], ident[:, :])

            def score_keys(u):
                i, heads = B_UNITS[u]
                if u >= 2:
                    pe.wait_ge(exped, u - 1)
                if u == B_FIRST[i]:
                    pe.wait_ge(max_placed[i % 2], 32 * (i // 2 + 1))
                bank = 2 + 2 * (u % 2)
                for jt in range(i + 1):
                    for n, h in enumerate(heads):
                        at = 512 * n + jt * P
                        last = pe.matmul(ps[:, bank + at // 512, at % 512:at % 512 + P],
                                         k_stack[0:ROWS, h, jt * P:(jt + 1) * P],
                                         q_stack[0:ROWS, i, h, :], start=True, stop=True)
                last.then_inc(scored, 1)

            def sum_values(u):
                i, heads = B_UNITS[u]
                if len(heads) == 1:
                    if u % 2 == 0:
                        return
                    heads = [heads[0] - 1, heads[0]]
                pe.wait_ge(exped, u + 1)
                if heads[0] == 0 and i:
                    pe.wait_ge(o_copied, i)
                for jt in range(i + 1):
                    if jt == i:
                        pe.wait_ge(masked, u + 1)
                    for n, h in enumerate(heads):
                        if i < 4:
                            p = probs[:, u % P_RING, 512 * n + jt * P:512 * n + (jt + 1) * P]
                        else:
                            p = probs[:, (u - 1 + n) % P_RING, jt * P:(jt + 1) * P]
                        c = 32 * (h % 4)
                        last = pe.matmul(ps[c:c + VW, 6, (h // 4) * P:(h // 4 + 1) * P], v_ext[:, jt, h, :], p,
                                         start=(jt == 0), stop=(jt == i))
                last.then_inc(summed, 1 if i < 4 else 2)

            def job(what, i):
                if turn[what, i]:
                    pe.wait_ge(misc_used, turn[what, i])
                if what == "max_turn":
                    last = turn_max(i)
                elif what == "o_turn":
                    pe.wait_ge(o_copied, i + 1)
                    for g in range(4):
                        last = pe.transpose(ps[:, 7, g * P:(g + 1) * P], o_sb[:, g, :], ident[:, :])
                elif what == "y_turn":
                    for c in range(DC):
                        last = pe.transpose(ps[:, 7, c * P:(c + 1) * P], y_tok[:, c * P:(c + 1) * P], ident[:, :])
                elif what == "proj":
                    pe.wait_ge(wp_loaded, 16)
                    for c in range(DC):
                        last = pe.matmul(ps[:, 7, D:2 * D], y_feat[:, c, :], wp_sb[:, c, :],
                                         start=(c == 0), stop=(c == DC - 1))
                elif what == "h_turn":
                    pe.wait_ge(h_ready, i + 1)
                    for c in range(DC):
                        last = pe.transpose(ps[:, 7, c * P:(c + 1) * P], h_tok[:, i, c * P:(c + 1) * P], ident[:, :])
                elif what == "logits":
                    for c in range(DC):
                        last = pe.matmul(ps[:, 7, D:D + EXPERTS], h_feat[:, c, i * P:(i + 1) * P], router_feat[:, c, :],
                                         start=(c == 0), stop=(c == DC - 1))
                elif what == "rank":
                    pe.wait_ge(chosen_ready, i + 1)
                    last = pe.matmul(ps[:, 7, 0:EXPERTS], before_b[:, :], chosen[:, i, :], start=True, stop=(i == 0))
                    for t in range(i):
                        last = pe.matmul(ps[:, 7, 0:EXPERTS], ones_b[:, :], chosen[:, t, :], start=False, stop=(t == i - 1))
                    if i >= PAD_TILE:
                        for t in range(i + 1):
                            last = pe.matmul(ps[:, 7, EXPERTS:2 * EXPERTS], ones_b[:, :], chosen[:, t, :],
                                             start=(t == 0), stop=(t == i))
                last.then_inc(misc_made, 1)

            def up(n, half):
                chunk, inner = n // 2, n % 2
                if (n, half) == (0, 0):
                    pe.wait_ge(shared_loaded, 48)
                    pe.wait_ge(row_maxed, len(A_UNITS))
                    pe.wait_ge(exped, NB)
                if n >= 2:
                    pe.wait_ge(shared_ready, n - 1)
                w = (sg_sb, su_sb)[half]
                for c in range(DC):
                    last = pe.matmul(ps[:, 2 * (n % 2) + half, :], w[:, c, inner * P:(inner + 1) * P],
                                     h_feat[:, c, chunk * 512:(chunk + 1) * 512], start=(c == 0), stop=(c == DC - 1))
                if half:
                    last.then_inc(shared_up, 1)

            def shared_out(t):
                if t % 4 == 0:
                    pe.wait_ge(shared_ready, 2 * (t // 4) + 2)
                if t >= 2:
                    pe.wait_ge(shared_added, t - 1)
                for c in range(2):
                    last = pe.matmul(ps[:, (6, 4)[t % 2], 0:D], shared_act[:, c, t * P:(t + 1) * P],
                                     sd_sb[:, c, :], start=(c == 0), stop=(c == 1))
                last.then_inc(shared_down, 1)

            job("max_turn", 0)
            pe.wait_ge(sums_cleared, 1)
            for a in range(EARLY, A_LAST[2] + 1):
                score_rows(a)
            score_keys(0)
            for u in range(STEPS):
                if u + 1 < NB:
                    score_keys(u + 1)
                for a in a_at[u]:
                    score_rows(a)
                if 1 <= u <= NB:
                    sum_values(u - 1)
                for what, i in pe_at[u]:
                    job(what, i)
                if u in pe_fill:
                    up(*pe_fill[u][1:])

            shared_out(0)
            shared_out(1)
            up(2, 0)
            up(2, 1)
            pe.wait_ge(cols_ready, 2)
            for n in range(2):
                last = pe.transpose(ps[0:1, 7, n * P:(n + 1) * P], block_cols[:, n:n + 1], ident[:, :])
            last.then_inc(cols_turned, 1)
            up(3, 0)
            up(3, 1)
            for t in range(2, TILES):
                shared_out(t)

            def fill_table():
                table = ps[:, 5, 0:MAX_BLOCKS]
                pe.wait_ge(act_feat_ready, TABLE_STEP)
                pe.wait_ge(positions_ready, 2)
                pe.wait_ge(places_scaled[0], 1)
                pe.wait_ge(places_scaled[1], 1)
                for n in range(TILES * TOPK):
                    for half in range(2):
                        last = pe.matmul(table, pos_onehot[:, n, :], block_row[:, half, n, :], start=(n + half == 0),
                                         stop=(n + half == TILES * TOPK))
                last.then_inc(rows_found, 1)

            pe.wait_ge(w1_loaded, 16 * DC)
            pe.wait_ge(w2_loaded, 16 * TILES)
            pe.wait_ge(offsets_ready, 2)
            pe.wait_ge(shared_ready, 4)

            def turn_x(b, n, r, q):
                pe.wait_ge(xs_loaded[r], 16 * q + 16)
                for c in range(DC):
                    last = pe.transpose(ps[:, 2 + n % 2, c * P:(c + 1) * P], xs_tok[:, r, c * P:(c + 1) * P], ident[:, :])
                last.then_inc(xs_turned, 1)

            offsets = [pe.alloc_register(f"offset{n}") for n in range(2 * RING)]

            def group(b):
                pe.load(offsets, w_off[0:1, bass.ds(b - RING + OFF_PAD, 2 * RING)])

            def offset(back):
                return pe.snap(offsets[RING + back], min_val=0, max_val=(EXPERTS - 1) * D)

            def step(b, n, r, q):
                g = (r - (RING - 1)) % RING
                if g == 0:
                    group(b)
                if n < MAX_BLOCKS:
                    at = offset(g)
                    pe.wait_ge(xs_ready, b + 1)
                    for c in range(DC):
                        last = pe.matmul(ps[:, n % 2, 0:D], xs_feat[:, r, c, :], w1_sb[:, bass.ds(at + c * EXPERTS * D, D)],
                                         start=(c == 0), stop=(c == DC - 1))
                    last.then_inc(gate_up, 1)
                if 1 <= n <= MAX_BLOCKS:
                    pe.wait_ge(act_ready, b)
                    pe.transpose(ps[:, 4 + (n - 1) % 2, 0:P], act_sb[:, (r - 1) % RING, :], ident[:, :]).then_inc(act_turned, 1)
                if n + 2 < MAX_BLOCKS:
                    turn_x(b + 2, n + 2, (r + 2) % RING, q + int(r >= RING - 2))
                if n >= 2:
                    at = offset(g - 2)
                    pe.wait_ge(act_feat_ready, b - 1)
                    pe.matmul(ps[:, 6 + n % 2, 0:D], act_feat[:, (r - 2) % RING, :], w2_sb[:, bass.ds(at, D)],
                              start=True, stop=True).then_inc(down, 1)
                if n == TABLE_STEP:
                    fill_table()

            turn_x(0, 0, 0, 0)
            turn_x(1, 1, 1, 0)
            group(-1)
            over_blocks(pe, step)

        @block.scalar
        def _(act):
            act.wait_ge(router_turned, 1)
            act.activation(router_feat[:, :, :].rearrange("p c e -> p (c e)"), ps[:, 7, 0:DC * EXPERTS],
                           ACT.Copy).then_inc(router_ready, 1)

            def turn_xn_copy(j):
                act.wait_ge(xn_turned, j + 1)
                act.activation(xn_feat[:, :, j * P:(j + 1) * P],
                               ps[:, 0, 0:D].rearrange("p (c q) -> p c q", c=DC), ACT.Copy).then_inc(xn_feat_ready, 1)

            turn_xn_copy(0)
            for j in range(TILES + 1):
                if j + 1 < TILES:
                    turn_xn_copy(j + 1)
                if j < TILES:
                    act.wait_ge(qk_made, j + 1)
                    if j == 0:
                        act.wait_ge(stack_consts, 1)
                    if j >= 2:
                        act.wait_ge(stacked[1], 2 * (j - 1))
                    for heads, first, step, scale in ((queries, 0, 1, QK_SCALE), (keys, 1, 2, 1.0)):
                        act.activation(part(j, heads, first, 3, step),
                                       ps[:, 2 + j % 2, heads.start * HD:heads.stop * HD].rearrange(
                                           "p (h d) -> p h d", d=HD).unsqueeze(2).broadcast_to([P, HEADS, 3, HD]),
                                       ACT.Copy, scale=scale).then_inc(a_ready, 1)
                if j:
                    for g, dst in enumerate((q_stack[:, j - 1, :, :], k_stack[:, :, (j - 1) * P:j * P])):
                        act.wait_ge(stacked[0], 2 * (j - 1) + g + 1)
                        act.activation(dst[0:ROWS, 0:8, :],
                                       ps[0:ROWS, 6, :].bitcast(BF16).rearrange("p (h q) -> p h q", h=8),
                                       ACT.Copy).then_inc(stack_ready[0], 1)

            def exp(u):
                i, heads = B_UNITS[u]
                act.wait_ge(scored, u + 1)
                if u >= P_RING:
                    act.wait_ge(summed, u - P_RING + 1)
                bank = 2 + 2 * (u % 2)
                if len(heads) == 2:
                    n = (i + 1) * P
                    act.activation(probs[:, u % P_RING, :].rearrange("p (a q) -> p a q", a=2)[:, :, 0:n],
                                   ps[:, bank:bank + 2, 0:n], ACT.Exp).then_inc(exped, 1)
                else:
                    n = (i + 1) * P
                    act.activation(probs[:, u % P_RING, 0:n],
                                   ps[:, bank:bank + 2, :].rearrange("p a q -> p (a q)")[:, 0:n], ACT.Exp).then_inc(exped, 1)

            def job(what, i):
                if what == "h_raw":
                    act.wait_ge(norm_ready, i + 1)
                    if i:
                        act.wait_ge(h_ready, i)
                    act.activation(h_raw[:, :], x_sb[:, i, :], ACT.Identity, bias=shift2[:, i % 2, 1:2],
                                   scale=rstd2[:, i % 2, 1:2]).then_inc(h_raw_ready, 1)
                    return
                if what == "base":
                    act.wait_ge(h_raw_ready, i + 1)
                    act.activation(base[:, i, :], x_sb[:, i, :], ACT.Identity, bias=shift2[:, i % 2, 0:1],
                                   scale=scale_base[:, i % 2, :]).then_inc(base_ready, 1)
                    return
                act.wait_ge(misc_made, turn[what.replace("copy", "turn"), i] + 1)
                dst = y_feat[:, :, :] if what == "y_copy" else h_feat[:, :, i * P:(i + 1) * P]
                act.activation(dst, ps[:, 7, 0:D].rearrange("p (c q) -> p c q", c=DC), ACT.Copy).then_inc(misc_used, 1)

            def silu(n):
                chunk, inner = n // 2, n % 2
                act.wait_ge(shared_up, n + 1)
                act.activation(shared_sig[:, inner, chunk * 512:(chunk + 1) * 512], ps[:, 2 * (n % 2), :],
                               ACT.Silu).then_inc(shared_silu, 1)

            for u in range(STEPS):
                for i in act_first[u]:
                    act.wait_ge(summed, B_FIRST[i + 1] if i + 1 < TILES else NB)
                    if i:
                        act.wait_ge(misc_made, turn["o_turn", i - 1] + 1)
                    act.activation(o_sb[:, :, :].rearrange("p g q -> p (g q)"), ps[:, 6, :], ACT.Copy).then_inc(o_copied, 1)
                if u < NB:
                    exp(u)
                for what, i in act_at[u]:
                    job(what, i)
                if u in act_fill:
                    silu(act_fill[u])
            act.wait_ge(top_ready, TILES)
            act.activation(top_e[:, :, :], top_d[:, :, :], ACT.Exp).then_inc(top_exped, 1)
            silu(2)
            silu(3)
            act.wait_ge(blocks_ready, 2)
            act.activation(block_row[:, 1, :, :], block_onehot[:, :, :], ACT.Copy, scale=partition[:, 0:1]).then_inc(places_scaled[1], 1)

            def step(b, n, r, q):
                if n < MAX_BLOCKS:
                    act.wait_ge(gate_up, b + 1)
                    act.activation(silu_sb[:, r, :], ps[:, n % 2, 0:P], ACT.Silu).then_inc(silu_ready, 1)
                if n + 2 < MAX_BLOCKS:
                    turn_x_copy(b + 2, n + 2, (r + 2) % RING)

            def turn_x_copy(b, n, r):
                act.wait_ge(xs_turned, b + 1)
                act.activation(xs_feat[:, r, :, :].rearrange("p c q -> p (c q)"), ps[:, 2 + n % 2, 0:D],
                               ACT.Copy).then_inc(xs_ready, 1)

            turn_x_copy(0, 0, 0)
            turn_x_copy(1, 1, 1)
            over_blocks(act, step)

        @block.vector
        def _(dve):
            steps = [0]

            def link(ins):
                steps[0] += 1
                ins.then_inc(dve_step, 1)
                dve.wait_ge(dve_step, steps[0])

            def note(ins):
                steps[0] += 1
                ins.then_inc(dve_step, 1)

            note(dve.memset(qk_tok[:, :, 0:HEADS, 0:2], 0.0))
            dve.memset(qk_tok[:, :, HEADS:2 * HEADS, 0:2], 1.0).then_inc(stack_consts, 1)
            for g in range(2):
                for j in range(4 * g, 4 * g + 4):
                    dve.wait_ge(x_loaded[j // 2], 16)
                    note(dve.bn_stats(stats[:, j, :], x_sb[:, j, :]))
                dve.wait_ge(dve_step, steps[0])
                for j in range(4 * g, 4 * g + 4):
                    note(dve.bn_aggr(mean_var[:, j, :], stats[:, j, :]))
                dve.wait_ge(dve_step, steps[0])
                dve.tensor_scalar(var_eps[:, 4 * g:4 * g + 4], mean_var[:, 4 * g:4 * g + 4, 1], EPS_LN, None,
                                  ALU.add).then_inc(stats_ready, 1)

            def normalise(j):
                dve.wait_ge(rstd_ready, j // 4 + 1)
                dve.tensor_scalar(xn[:, j, :], x_sb[:, j, :], mean_var[:, j, 0:1], rstd[:, j:j + 1],
                                  ALU.subtract, ALU.mult).then_inc(xn_ready, 1)

            def maximum(a):
                i, heads, k0, kw, part, _ = A_UNITS[a]
                dve.wait_ge(rows_scored, a + 1)
                dve.tensor_reduce(row_max[:, part, i, heads[0]:heads[-1] + 1],
                                  ps[:, 1 if a < EARLY else a % 2, 0:len(heads) * kw].rearrange("p (h k) -> p h k", h=len(heads)),
                                  X, ALU.max).then_inc(row_maxed, 1)

            normalise(0)
            normalise(1)
            for j in range(TILES + 1):
                if j + 2 < TILES:
                    normalise(j + 2)
                for a in early[j, 0]:
                    maximum(a)
                if j < TILES:
                    dve.wait_ge(a_ready, 2 * (j + 1))
                    if j >= 2:
                        dve.wait_ge(b_ready, j - 1)
                    for heads, scale in ((queries, QK_SCALE), (keys, 1.0)):
                        dve.scalar_tensor_tensor(out=rest[:, j % 2, heads, :],
                                                 in0=ps[:, 2 + j % 2, heads.start * HD:heads.stop * HD].rearrange(
                                                     "p (h d) -> p h d", d=HD), scalar=scale,
                                                 in1=qk_tok[:, j % 2, heads, 2 + HD:2 + 2 * HD],
                                                 op0=ALU.mult, op1=ALU.subtract).then_inc(rest_ready, 1)
                    dve.wait_ge(v_made, j + 1)
                    if j == 0:
                        dve.wait_ge(consts, 1)
                    dve.tensor_copy(v_ext[:, j, :, 0:HD],
                                    ps[:, 4 + j % 2, 0:D].rearrange("p (h d) -> p h d", h=HEADS)).then_inc(v_ready, 1)
                    for a in early[j, 1]:
                        maximum(a)
                if j:
                    for g, dst in enumerate((q_stack[:, j - 1, :, :], k_stack[:, :, (j - 1) * P:j * P])):
                        dve.wait_ge(stacked[1], 2 * (j - 1) + g + 1)
                        dve.tensor_copy(dst[0:ROWS, 8:16, :],
                                        ps[0:ROWS, 7, :].bitcast(BF16).rearrange("p (h q) -> p h q", h=8)
                                        ).then_inc(stack_ready[1], 1)
                        for a in early[j, 2 + g]:
                            maximum(a)
                if j < TILES:
                    dve.wait_ge(rest_ready, 2 * (j + 1))
                    dve.wait_ge(b_ready, j + 1)
                    b_at, at = 2 + 4 * HD, {0: 2 + 5 * HD, HEADS: 2}
                    for h in (0, HEADS):
                        dve.tensor_tensor(qk_tok[:, j % 2, h:h + HEADS, at[h]:at[h] + HD], rest[:, j % 2, h:h + HEADS, :],
                                          qk_tok[:, j % 2, h:h + HEADS, b_at:b_at + HD], ALU.subtract).then_inc(c_ready, 1)

            for g in range(2):
                dve.wait_ge(stack_ready[g], 2 * TILES)
            dve.memset(ps[:, 6, :], 0.0).then_inc(sums_cleared, 1)

            def job(what, i):
                if what == "max_join":
                    dve.wait_ge(row_maxed, A_LAST[i] + 1)
                    dve.tensor_tensor(row_max[:, 0, i, :], row_max[:, 0, i, :], row_max[:, 1, i, :],
                                      ALU.max).then_inc(max_joined, 1)
                elif what == "max_copy":
                    dve.wait_ge(misc_made, turn["max_turn", i] + 1)
                    if i >= 2:
                        dve.wait_ge(max_placed[i % 2], 32 * (i // 2))
                    link(dve.tensor_scalar(neg_max[:, i % 2, 0, :], ps[0:HEADS, 7, 0:P], -1.0, None, ALU.mult))
                    dve.scalar_tensor_tensor(out=neg_max[:, i % 2, 1, :], in0=ps[0:HEADS, 7, 0:P], scalar=-1.0,
                                             in1=neg_max[:, i % 2, 0, :], op0=ALU.mult,
                                             op1=ALU.subtract).then_inc(misc_used, 1)
                elif what == "norm":
                    dve.wait_ge(misc_made, turn["o_turn", i] + 1)
                    sums = ps[:, 7, :].rearrange("p (h c) -> p h c", h=HEADS)
                    if i:
                        dve.wait_ge(misc_made, turn["y_turn", i - 1] + 1)
                    link(dve.reciprocal(denom[:, :], sums[:, :, HD]))
                    dve.tensor_tensor(y_tok[:, :].rearrange("p (h d) -> p h d", h=HEADS), sums[:, :, 0:HD],
                                      denom[:, :].unsqueeze(2).broadcast_to([P, HEADS, HD]), ALU.mult).then_inc(misc_used, 1)
                elif what == "residual":
                    dve.wait_ge(misc_made, turn["proj", i] + 1)
                    x_i = x_sb[:, i, :]
                    ins = dve.tensor_tensor(x_i, x_i, ps[:, 7, D:2 * D], ALU.add)
                    ins.then_inc(misc_used, 1)
                    dve.wait_ge(misc_used, turn["proj", i] + 1)
                    link(dve.bn_stats(stats2[:, :], x_i))
                    if i >= 2:
                        dve.wait_ge(base_ready, i - 1)
                    link(dve.bn_aggr(mean_var2[:, i % 2, :], stats2[:, :]))
                    var = mean_var2[:, i % 2, 1:2]
                    link(dve.tensor_scalar(var_args[:, i % 2, 0:1], var, EPS_LN, None, ALU.add))
                    dve.scalar_tensor_tensor(out=var_args[:, i % 2, 1:2], in0=var_args[:, i % 2, 0:1], scalar=EPS_RMS,
                                             in1=var, op0=ALU.mult, op1=ALU.add).then_inc(var_ready, 1)
                elif what == "h":
                    dve.wait_ge(h_raw_ready, i + 1)
                    if i == 0:
                        dve.wait_ge(nw_loaded, 16)
                    dve.tensor_tensor(h_tok[:, i, :], h_raw[:, :], nw_sb[:, :], ALU.mult).then_inc(h_ready, 1)
                    dve.wait_ge(h_ready, i + 1)
                elif what == "top":
                    dve.wait_ge(misc_made, turn["logits", i] + 1)
                    dve.tensor_copy(logit_sb[:, i, :], ps[:, 7, D:D + EXPERTS]).then_inc(misc_used, 1)
                    dve.wait_ge(misc_used, turn["logits", i] + 1)
                    link(dve.max(top_v[:, i, :], logit_sb[:, i, :]))
                    note(dve.max_index(top_i[:, i, :], top_v[:, i, :], logit_sb[:, i, :]))
                    dve.tensor_scalar(top_d[:, i, :], top_v[:, i, 0:TOPK], top_v[:, i, 0:1], None,
                                      ALU.subtract).then_inc(top_ready, 1)
                    dve.wait_ge(dve_step, steps[0])
                    link(dve.tensor_copy(idx_f[:, i, :], top_i[:, i, 0:TOPK]))
                    link(dve.tensor_tensor(onehot[:, i, :, :], iota_e.unsqueeze(1).broadcast_to([P, TOPK, EXPERTS]),
                                           idx_f[:, i, :].unsqueeze(2).broadcast_to([P, TOPK, EXPERTS]), ALU.is_equal))
                    with nc.allow_low_precision(reason="a token chooses an expert once or not: 0 or 1"):
                        dve.tensor_reduce(chosen[:, i, :], onehot[:, i, :, :].rearrange("p k e -> p e k"),
                                          X, ALU.add).then_inc(chosen_ready, 1)
                elif what == "slot":
                    dve.wait_ge(misc_made, turn["rank", i] + 1)
                    if i == PAD_TILE:
                        dve.tensor_tensor(pad_i[:, :], ps[0:1, 7, EXPERTS:2 * EXPERTS], region_base[0:1, :],
                                          ALU.add).then_inc(pads_ready, 1)
                    dve.tensor_tensor(slot_te[:, :], ps[:, 7, 0:EXPERTS], region_base[:, :], ALU.add).then_inc(misc_used, 1)
                    dve.wait_ge(misc_used, turn["rank", i] + 1)
                    link(dve.tensor_tensor(slot_of[:, :, :], onehot[:, i, :, :],
                                           slot_te[:, :].unsqueeze(1).broadcast_to([P, TOPK, EXPERTS]), ALU.mult))
                    link(dve.tensor_reduce(slot_f[:, i, :], slot_of[:, :, :], X, ALU.add))
                    dve.tensor_copy(slot_i[:, TOPK * i:TOPK * (i + 1)], slot_f[:, i, :]).then_inc(slots_ready, 1)

            def shared(n):
                chunk, inner = n // 2, n % 2
                cols = slice(chunk * 512, (chunk + 1) * 512)
                dve.wait_ge(shared_silu, n + 1)
                dve.tensor_tensor(shared_act[:, inner, cols], shared_sig[:, inner, cols], ps[:, 2 * (n % 2) + 1, :],
                                  ALU.mult).then_inc(shared_ready, 1)

            pairs = TILES * TOPK

            def positions(t0, t1):
                some = slice(t0 * TOPK, t1 * TOPK)
                n = some.stop - some.start
                dve.wait_ge(slots_ready, t1)
                link(dve.tensor_scalar(place[:, some], slot_i[:, some], P - 1, None, ALU.bitwise_and))
                link(dve.tensor_copy(place_f[:, some], place[:, some]))
                dve.tensor_tensor(pos_onehot[:, some, :], iota_row[:, :].unsqueeze(1).broadcast_to([P, n, P]),
                                  place_f[:, some].unsqueeze(2).broadcast_to([P, n, P]),
                                  ALU.is_equal).then_inc(positions_ready, 1)

            job("max_copy", 0)
            for a in range(EARLY, A_LAST[2] + 1):
                maximum(a)
            for u in range(STEPS):
                for what, i in dve_at[u]:
                    job(what, i)
                if u < NB:
                    for a in a_at[u]:
                        maximum(a)
                if u in dve_fill:
                    {"shared": shared, "positions": positions}[dve_fill[u][0]](*dve_fill[u][1:])

            dve.wait_ge(misc_made, turn["rank", TILES - 1] + 1)
            counts = ps[:, 7, EXPERTS:2 * EXPERTS]
            link(dve.tensor_scalar(count_i[:, 0:EXPERTS], counts, float(P - 1), None, ALU.add))
            link(dve.tensor_scalar(count_i[:, EXPERTS:], count_i[:, 0:EXPERTS], 7, None, ALU.arith_shift_right))
            link(dve.tensor_copy(nblk[:, :], count_i[:, EXPERTS:]))
            note(dve.tensor_scalar(rows_less[:, :], nblk[:, :], -float(P), float(REGION), ALU.mult, ALU.add))
            link(dve.tensor_tensor_scan(nblk_end[:, :], nblk[:, :], zeros[:, 0:EXPERTS], 0.0, ALU.add, ALU.add))
            note(dve.tensor_tensor(nblk_start[:, :], nblk_end[:, :], nblk[:, :], ALU.subtract))
            link(dve.tensor_scalar(below[:, :], nblk_end[:, :], partition[:, 0:1], None, ALU.is_le))
            note(dve.tensor_reduce(block_cols[:, 2:3], below[:, :], X, ALU.add))
            link(dve.tensor_tensor(below_rows[:, :], below[:, :], rows_less[:, :], ALU.mult))
            link(dve.tensor_reduce(block_cols[:, 3:4], below_rows[:, :], X, ALU.add))
            dve.tensor_scalar(block_cols[:, 0:1], block_cols[:, 2:3], float(EXPERTS - 1), float(D), ALU.min,
                              ALU.mult).then_inc(cols_ready, 1)
            link(dve.scalar_tensor_tensor(out=block_cols[:, 3:4], in0=partition[:, :], scalar=float(P),
                                          in1=block_cols[:, 3:4], op0=ALU.mult, op1=ALU.add))
            dve.tensor_scalar(block_cols[:, 1:2], block_cols[:, 3:4], float(ZERO_ROW), None, ALU.min).then_inc(cols_ready, 1)
            note(dve.memset(w_off[:, :], 0))
            link(dve.memset(x_row[:, :], 0))

            def add_shared(t):
                dve.wait_ge(shared_down, t + 1)
                dve.wait_ge(base_ready, t + 1)
                dve.tensor_tensor(base[:, t, :], base[:, t, :], ps[:, (6, 4)[t % 2], 0:D],
                                  ALU.add).then_inc(shared_added, 1)

            add_shared(0)
            add_shared(1)
            positions(TILES // 2, TILES)
            dve.wait_ge(cols_turned, 1)
            dve.tensor_copy(w_off[:, OFF_PAD:OFF_PAD + MAX_BLOCKS], ps[0:1, 7, 0:MAX_BLOCKS]).then_inc(offsets_ready, 1)
            dve.tensor_copy(x_row[:, 1:1 + MAX_BLOCKS], ps[0:1, 7, P:P + MAX_BLOCKS]).then_inc(offsets_ready, 1)

            note(dve.tensor_scalar(place[:, pairs:], slot_i[:, :], 7, None, ALU.arith_shift_right))
            link(dve.scalar_tensor_tensor(out=nblk_start[:, :], in0=region_base[:, :], scalar=-1.0 / P,
                                          in1=nblk_start[:, :], op0=ALU.mult, op1=ALU.add))
            link(dve.tensor_tensor(pair_start[:, :, :], onehot[:, :, :, :].rearrange("p t k e -> p (t k) e"),
                                   nblk_start[:, :].unsqueeze(1).broadcast_to([P, pairs, EXPERTS]), ALU.mult))
            shared(2)
            link(dve.tensor_reduce(pair_first[:, :], pair_start[:, :, :], X, ALU.add))
            link(dve.tensor_tensor(place_f[:, pairs:], place[:, pairs:], pair_first[:, :], ALU.add))
            shared(3)
            for t in range(2, TILES):
                if t in (3, 4):
                    some = slice((t - 3) * (pairs // 2), (t - 2) * (pairs // 2))
                    dve.tensor_tensor(block_onehot[:, some, :],
                                      iota_row[:, 0:MAX_BLOCKS].unsqueeze(1).broadcast_to([P, pairs // 2, MAX_BLOCKS]),
                                      place_f[:, pairs + some.start:pairs + some.stop].unsqueeze(2).broadcast_to(
                                          [P, pairs // 2, MAX_BLOCKS]), ALU.is_equal).then_inc(blocks_ready, 1)
                add_shared(t)

            def step(b, n, r, q):
                if 1 <= n <= MAX_BLOCKS:
                    dve.wait_ge(act_turned, b)
                    dve.tensor_copy(act_feat[:, (r - 1) % RING, :], ps[:, 4 + (n - 1) % 2, 0:P]).then_inc(act_feat_ready, 1)
                if n == TABLE_STEP + 1:
                    dve.wait_ge(rows_found, 1)
                    table = ps[:, 5, 0:MAX_BLOCKS]
                    link(dve.scalar_tensor_tensor(out=unused[:, :], in0=table, scalar=float(P), in1=spare_row[:, :],
                                                  op0=ALU.is_lt, op1=ALU.mult))
                    dve.scalar_tensor_tensor(out=row_i[:, :], in0=table, scalar=-float(P), in1=unused[:, :],
                                             op0=ALU.add, op1=ALU.add).then_inc(rows_ready, 1)
                if n < MAX_BLOCKS:
                    dve.wait_ge(silu_ready, b + 1)
                    dve.tensor_tensor(act_sb[:, r, :], silu_sb[:, r, :], ps[:, n % 2, P:2 * P], ALU.mult).then_inc(act_ready, 1)
                if n >= 2:
                    r2 = (r - 2) % RING
                    dve.wait_ge(down, b - 1)
                    if n - 2 >= RING:
                        dve.wait_ge(ys_stored[r2], 16 * (q if r >= 2 else q - 1))
                    dve.tensor_copy(ys_sb[:, r2, :], ps[:, 6 + n % 2, 0:D]).then_inc(ys_ready, 1)

            over_blocks(dve, step)

            dve.wait_ge(top_exped, 1)
            link(dve.tensor_reduce(top_sum[:, :], top_e[:, :, :], X, ALU.add))
            link(dve.reciprocal(top_sum[:, :], top_sum[:, :]))
            link(dve.tensor_tensor(top_w[:, :, :], top_e[:, :, :],
                                   top_sum[:, :].unsqueeze(2).broadcast_to([P, TILES, TOPK]), ALU.mult))
            for t in range(TILES):
                dve.wait_ge(row_gathered[t], 16)
                for k in range(TOPK):
                    ins = dve.scalar_tensor_tensor(out=base[:, t, :], in0=gathered[:, TOPK * t + k, :],
                                                   scalar=top_w[:, t, k:k + 1], in1=base[:, t, :],
                                                   op0=ALU.mult, op1=ALU.add)
                    if k < TOPK - 1:
                        link(ins)
                    else:
                        ins.then_inc(combined, 1)


_INS = ["L0_attn_x", "L0_attn_w_attn", "L0_attn_w_proj", "L0_ffn_norm_w", "L0_ffn_router_w", "L0_ffn_w1",
        "L0_ffn_w2", "L0_ffn_sg", "L0_ffn_su", "L0_ffn_sd"]


def kernel(**inputs):
    import numpy as _np
    import concourse.bacc as _bacc
    from concourse import mybir as _mybir
    from concourse.bass_utils import run_bass_kernel_spmd as _run

    nc = _bacc.Bacc("TRN2", target_bir_lowering=False, num_devices=1)
    arrays, args = {}, []
    for name in _INS:
        a = _np.ascontiguousarray(inputs[name])
        arrays[f"in_{name}"] = a
        args.append(nc.dram_tensor(f"in_{name}", a.shape, _mybir.dt.from_np(a.dtype), kind="ExternalInput").ap())
    args.append(nc.dram_tensor("out_x", (1, T, D), F32, kind="ExternalOutput").ap())
    layer(nc, *args)
    r = _run(nc, [arrays], core_ids=[0])
    return r.results[0]["out_x"]
```
